# Optimizing a Trainium2 kernel written in Bass

```python
import numpy as np
import jax
import jax.numpy as jnp

def _softmax(x, axis=-1):
    return jax.nn.softmax(x, axis=axis)

def _gelu(x):
    return jax.nn.gelu(x, approximate=True)

def _silu(x):
    return jax.nn.silu(x)

def _sigmoid(x):
    return jax.nn.sigmoid(x)

def _layernorm(x, axis=-1, eps=1e-05):
    m = jnp.mean(x, axis=axis, keepdims=True)
    v = jnp.var(x, axis=axis, keepdims=True)
    return (x - m) / jnp.sqrt(v + eps)

def _scatter_add(tgt, idx, src, axis=0):
    return tgt.at[idx].add(src)

def _segment_sum(src, seg, n):
    return jax.ops.segment_sum(src, seg, n)
kernel_name = 'mk_macaron_d1_jaxref_r4_ecf8da'

def setup_inputs(seed: int=0):
    np.random.seed(seed)
    _w = jnp.asarray

    def _L0_attn_setup():
        import jax, jax.numpy as jnp
        import numpy as np
        B, T, C = (1, 1024, 512)
        H = 16
        D = C // H
        BLOCK = 64
        WINDOW = 256
        DILATION = 64
        GLOBAL_TOKENS = 128
        ROPE_BASE = 10000.0
        SCALE = 1.0 / np.sqrt(D)

        def _rope(x):
            t = jnp.arange(x.shape[2], dtype=jnp.float32)
            inv_freq = 1.0 / ROPE_BASE ** (jnp.arange(0, D, 2, dtype=jnp.float32) / D)
            freqs = jnp.outer(t, inv_freq)
            emb = jnp.concatenate([freqs, freqs], axis=-1)
            cos = jnp.cos(emb)[None, None].astype(x.dtype)
            sin = jnp.sin(emb)[None, None].astype(x.dtype)
            x1, x2 = jnp.split(x, 2, axis=-1)
            rot = jnp.concatenate([-x2, x1], axis=-1)
            return x * cos + rot * sin

        def _token_mask(seq_len):
            nb = (seq_len + BLOCK - 1) // BLOCK
            bp = jnp.arange(nb)
            qb, kb = (bp[:, None], bp[None, :])
            dist = qb - kb
            window_blocks = WINDOW // BLOCK
            window_mask = (dist >= 0) & (dist <= window_blocks)
            global_blocks = max(1, GLOBAL_TOKENS // BLOCK)
            global_mask = kb < global_blocks
            dilation_blocks = max(1, DILATION // BLOCK)
            dilated_mask = kb % dilation_blocks == 0
            causal_mask = kb <= qb
            block_mask = (window_mask | global_mask | dilated_mask) & causal_mask
            tok = jnp.repeat(jnp.repeat(block_mask, BLOCK, axis=0), BLOCK, axis=1)
            return tok[:seq_len, :seq_len]
        key = jax.random.key(seed)
        ks = jax.random.split(key, 5)
        x = jax.random.normal(ks[0], (B, T, C), dtype=jnp.float32)
        w_q = jax.random.normal(ks[1], (C, C), dtype=jnp.float32) * 0.02
        w_k = jax.random.normal(ks[2], (C, C), dtype=jnp.float32) * 0.02
        w_v = jax.random.normal(ks[3], (C, C), dtype=jnp.float32) * 0.02
        w_o = jax.random.normal(ks[4], (C, C), dtype=jnp.float32) * 0.02
        return {'x': x, 'w_q': w_q, 'w_k': w_k, 'w_v': w_v, 'w_o': w_o}
    _L0_attn_in = _L0_attn_setup()

    def _L0_ffn_setup():
        import jax, jax.numpy as jnp
        import numpy as np
        LN_EPS = 1e-05
        Q_EPS = 1e-05

        def ternary_quantize(w):
            scale = jnp.mean(jnp.abs(w))
            return jnp.clip(jnp.round(w / (scale + Q_EPS)), -1.0, 1.0)

        def layernorm(x, gamma, beta):
            mu = jnp.mean(x, axis=-1, keepdims=True)
            var = jnp.mean(jnp.square(x - mu), axis=-1, keepdims=True)
            return (x - mu) * jax.lax.rsqrt(var + LN_EPS) * gamma + beta
        key = jax.random.key(seed)
        k_x, k_w = jax.random.split(key)
        B, S, D_IN, D_OUT = (4, 512, 512, 512)
        x = jax.random.normal(k_x, (B, S, D_IN), dtype=jnp.float32)
        std = np.sqrt(2.0 / D_OUT).astype(np.float32)
        weight = jax.random.normal(k_w, (D_OUT, D_IN), dtype=jnp.float32) * std
        bias = jnp.zeros((D_OUT,), dtype=jnp.float32)
        ln_gamma = jnp.ones((D_IN,), dtype=jnp.float32)
        ln_beta = jnp.zeros((D_IN,), dtype=jnp.float32)
        return {'x': x, 'weight': weight, 'bias': bias, 'ln_gamma': ln_gamma, 'ln_beta': ln_beta}
    _L0_ffn_in = _L0_ffn_setup()
    _d = {'L0_attn_x': _L0_attn_in['x'], 'L0_attn_w_q': _L0_attn_in['w_q'], 'L0_attn_w_k': _L0_attn_in['w_k'], 'L0_attn_w_v': _L0_attn_in['w_v'], 'L0_attn_w_o': _L0_attn_in['w_o'], 'L0_ffn_weight': _L0_ffn_in['weight'], 'L0_ffn_bias': _L0_ffn_in['bias'], 'L0_ffn_ln_gamma': _L0_ffn_in['ln_gamma'], 'L0_ffn_ln_beta': _L0_ffn_in['ln_beta']}
    _x0 = _d['L0_attn_x']
    _d['L0_attn_x'] = jax.random.normal(jax.random.fold_in(jax.random.key(seed), 1), (2, 1024, 512), dtype=_x0.dtype)
    del _x0
    return _d

def reference(L0_attn_x, L0_attn_w_q, L0_attn_w_k, L0_attn_w_v, L0_attn_w_o, L0_ffn_weight, L0_ffn_bias, L0_ffn_ln_gamma, L0_ffn_ln_beta):

    def _L0_attn_ref(x, w_q, w_k, w_v, w_o):
        import jax, jax.numpy as jnp
        import numpy as np
        B, T, C = (1, 1024, 512)
        H = 16
        D = C // H
        BLOCK = 64
        WINDOW = 256
        DILATION = 64
        GLOBAL_TOKENS = 128
        ROPE_BASE = 10000.0
        SCALE = 1.0 / np.sqrt(D)

        def _rope(x):
            t = jnp.arange(x.shape[2], dtype=jnp.float32)
            inv_freq = 1.0 / ROPE_BASE ** (jnp.arange(0, D, 2, dtype=jnp.float32) / D)
            freqs = jnp.outer(t, inv_freq)
            emb = jnp.concatenate([freqs, freqs], axis=-1)
            cos = jnp.cos(emb)[None, None].astype(x.dtype)
            sin = jnp.sin(emb)[None, None].astype(x.dtype)
            x1, x2 = jnp.split(x, 2, axis=-1)
            rot = jnp.concatenate([-x2, x1], axis=-1)
            return x * cos + rot * sin

        def _token_mask(seq_len):
            nb = (seq_len + BLOCK - 1) // BLOCK
            bp = jnp.arange(nb)
            qb, kb = (bp[:, None], bp[None, :])
            dist = qb - kb
            window_blocks = WINDOW // BLOCK
            window_mask = (dist >= 0) & (dist <= window_blocks)
            global_blocks = max(1, GLOBAL_TOKENS // BLOCK)
            global_mask = kb < global_blocks
            dilation_blocks = max(1, DILATION // BLOCK)
            dilated_mask = kb % dilation_blocks == 0
            causal_mask = kb <= qb
            block_mask = (window_mask | global_mask | dilated_mask) & causal_mask
            tok = jnp.repeat(jnp.repeat(block_mask, BLOCK, axis=0), BLOCK, axis=1)
            return tok[:seq_len, :seq_len]
        Bc, Tc, Cc = x.shape
        q = (x @ w_q.T).reshape(Bc, Tc, H, D).transpose(0, 2, 1, 3)
        k = (x @ w_k.T).reshape(Bc, Tc, H, D).transpose(0, 2, 1, 3)
        v = (x @ w_v.T).reshape(Bc, Tc, H, D).transpose(0, 2, 1, 3)
        q = _rope(q)
        k = _rope(k)
        scores = jnp.einsum('bhqd,bhkd->bhqk', q, k) * SCALE
        tok_mask = _token_mask(Tc)
        scores = jnp.where(tok_mask[None, None], scores, -jnp.inf)
        attn = jax.nn.softmax(scores, axis=-1)
        ctx = jnp.einsum('bhqk,bhkd->bhqd', attn, v)
        ctx = ctx.transpose(0, 2, 1, 3).reshape(Bc, Tc, Cc)
        return ctx @ w_o.T

    def _L0_ffn_ref(x, weight, bias, ln_gamma, ln_beta):
        import jax, jax.numpy as jnp
        import numpy as np
        LN_EPS = 1e-05
        Q_EPS = 1e-05

        def ternary_quantize(w):
            scale = jnp.mean(jnp.abs(w))
            return jnp.clip(jnp.round(w / (scale + Q_EPS)), -1.0, 1.0)

        def layernorm(x, gamma, beta):
            mu = jnp.mean(x, axis=-1, keepdims=True)
            var = jnp.mean(jnp.square(x - mu), axis=-1, keepdims=True)
            return (x - mu) * jax.lax.rsqrt(var + LN_EPS) * gamma + beta
        xn = layernorm(x, ln_gamma, ln_beta)
        w_q = ternary_quantize(weight)
        return jnp.einsum('bsi,oi->bso', xn, w_q) + bias
    x = L0_attn_x
    x = x + 0.5 * _L0_ffn_ref(_layernorm(x, axis=-1), L0_ffn_weight, L0_ffn_bias, L0_ffn_ln_gamma, L0_ffn_ln_beta)
    x = x + _L0_attn_ref(_layernorm(x, axis=-1), L0_attn_w_q, L0_attn_w_k, L0_attn_w_v, L0_attn_w_o)
    x = x + 0.5 * _L0_ffn_ref(_layernorm(x, axis=-1), L0_ffn_weight, L0_ffn_bias, L0_ffn_ln_gamma, L0_ffn_ln_beta)
    return x

_drawn_inputs = setup_inputs


def setup_inputs(seed=0):
    import zlib

    import numpy as np

    out = dict(_drawn_inputs(seed))
    spreads = {'L0_ffn_bias': (0.0, 0.8), 'L0_ffn_ln_gamma': (1.0, 0.2), 'L0_ffn_ln_beta': (0.0, 0.1)}
    factors = {'L0_attn_w_q': 8.0, 'L0_attn_w_k': 8.0, 'L0_attn_w_v': 8.0, 'L0_attn_w_o': 8.0}
    for name, (base, spread) in spreads.items():
        noise = np.random.default_rng([zlib.crc32(name.encode()), seed]).standard_normal(out[name].shape)
        drawn = base * np.exp(spread * noise) if base else spread * noise
        out[name] = jnp.asarray(drawn.astype(out[name].dtype))
    for name, factor in factors.items():
        out[name] = (out[name] * factor).astype(out[name].dtype)
    return out
```

```python
from contextlib import ExitStack

import concourse.bass as bass
from concourse import mybir

F32 = mybir.dt.float32
F16 = mybir.dt.float16
ALU = mybir.AluOpType
ACT = mybir.ActivationFunctionType
AX = mybir.AxisListType

BATCH, T, C, HEADS = 2, 1024, 512, 16
D = C // HEADS
P = 128
TILES = T // P
CC = C // P
HALF = 512
BLOCKS = T // HALF
GH = P // D
GROUPS = HEADS // GH
SETS = 3
LN_EPS = 1e-5
Q_EPS = 1e-5
W_SCALE = 64.0
QK_SCALE = 16.0
CTX_SCALE = 16.0
EXP_SCALE = float(D) ** -0.5 / (QK_SCALE * QK_SCALE)
LSE_ROW = 2048.0
MASK_ROW = 3 * D
LSE_FIRST = MASK_ROW + TILES
ROWS_A = LSE_FIRST
ROWS_B = LSE_FIRST + 3

STEPS = 48
A_TILES = GH * TILES
B_ORDER = [(half, j) for half in range(BLOCKS) for j in range(4 * half + 4)]
PROJ_AT = [10 * m + 5 for m in range(4)]
LAST_STEP = STEPS * (GROUPS + 2) + 8
DVE_LINKS = 3 * TILES + 5 * HEADS


def macaron(nc, x, w_q, w_k, w_v, w_o, w_f, bias, gamma, beta, cos_t, sin_t, ident_in, ident16_in,
            q_rows, k_rows, out):
    ctx = ExitStack()
    with ctx:
        def sb(name, shape, dt):
            return ctx.enter_context(nc.sbuf_tensor(name, shape, dt))

        def sem(name):
            return ctx.enter_context(nc.semaphore(name))

        xs = sb("xs", [P, TILES, C], F32)
        xh = sb("xh", [P, CC, T], F16)
        xl = sb("xl", [P, CC, T], F16)
        vs = sb("vs", [P, TILES, C], F32)
        ch = sb("ch", [P, GROUPS, T], F16)
        cl = sb("cl", [P, GROUPS, T], F16)
        wh = sb("wh", [P, 4, CC, C], F16)
        wl = sb("wl", [P, 4, CC, C], F16)
        wt = sb("wt", [P, CC, C], F16)
        cos_s = sb("cos_s", [P, T], F32)
        sin_s = sb("sin_s", [P, T], F32)
        qst = sb("qst", [P, SETS, GH, T], F16)
        kst = sb("kst", [P, SETS, GH, T], F16)
        rh = sb("rh", [P, 2, HALF], F16)
        rl = sb("rl", [P, 2, HALF], F16)
        t1 = sb("t1", [P, 2, HALF], F32)
        fh = sb("fh", [P, CC, HALF], F16)
        fl = sb("fl", [P, CC, HALF], F16)
        big = sb("big", [P, 24 * 256], F32)
        y = big[:, 0:4096].rearrange("p (b t c) -> p b t c", b=2, t=4)
        f = big[:, 4096:6144].rearrange("p (c n) -> p c n", c=CC)
        probs = big[:, 0:4096].rearrange("p (s h n) -> p s h n", s=2, h=GH)
        raw = big[:, 4096:5120].rearrange("p (s n) -> p s n", s=2)
        rot = big[:, 5120:6144].rearrange("p (s n) -> p s n", s=2)
        stage = [vs[:, 0:4, :], vs[:, 4:8, :],
                 ch[:, :, :].rearrange("p g t -> p (g t)").bitcast(F32).rearrange("p (a b) -> p a b", a=4),
                 cl[:, :, :].rearrange("p g t -> p (g t)").bitcast(F32).rearrange("p (a b) -> p a b", a=4)]
        wf_s = xs[:, 0:4, :]
        wtg = xl[:, 0:2, :].rearrange("p a t -> p (a t)").rearrange("p (a b) -> p a b", a=4)
        biasb = sb("biasb", [P, C], F32)
        ident = sb("ident", [P, P], F32)
        ident16 = sb("ident16", [P, P], F16)
        ones = sb("ones", [P, P], F32)
        gam = sb("gam", [P, CC], F32)
        bet = sb("bet", [P, CC], F32)
        sums = sb("sums", [P, 4], F32)
        stats = sb("stats", [P, TILES, 6], F32)
        mv = sb("mv", [P, TILES, 2], F32)
        var_e = sb("var_e", [P, TILES], F32)
        half_neg = sb("half_neg", [P, TILES], F32)
        rstd = sb("rstd", [P, TILES], F32)
        rmax = sb("rmax", [P, GROUPS * A_TILES], F32)
        nmax = sb("nmax", [P, GROUPS * A_TILES], F32)
        rsum = sb("rsum", [P, GROUPS * A_TILES], F32)
        lsum = sb("lsum", [P, GROUPS * A_TILES], F32)
        lrow = sb("lrow", [P, 2, TILES], F32)
        lres = sb("lres", [P, 2, TILES], F32)
        lparts = sb("lparts", [P, 2, 3, TILES], F16)
        lrows = sb("lrows", [3 * TILES, 2, P], F16)
        hold = sb("hold", [P, 6], F32)

        ps = [ctx.enter_context(nc.psum_tensor(f"ps{i}", [P, HALF], F32)) for i in range(4, 8)]
        pa = [ctx.enter_context(nc.psum_tensor(f"pa{i}", [P, T], F32)) for i in range(2)]
        tr = [pa[0][:, 0:HALF], pa[0][:, HALF:T], pa[1][:, 0:HALF], pa[1][:, HALF:T]]
        pb = ps[0:2]
        acc = ps[2]
        pp = ps[3]

        s_const = sem("s_const")
        s_w = [sem(f"s_w{i}") for i in range(5)]
        s_rows = sem("s_rows")
        s_pool0 = sem("s_pool0")
        s_abs = sem("s_abs")
        s_tot = sem("s_tot")
        s_tern = sem("s_tern")
        s_wh = sem("s_wh")
        s_wl = sem("s_wl")
        s_x = [sem(f"s_x{i}") for i in range(BLOCKS)]
        s_link = sem("s_link")
        s_aggr = sem("s_aggr")
        s_var = sem("s_var")
        s_rstd = sem("s_rstd")
        s_y = sem("s_y")
        s_xb = sem("s_xb")
        s_ytr = sem("s_ytr")
        s_f = sem("s_f")
        s_fh = sem("s_fh")
        s_fl = sem("s_fl")
        s_ffn = sem("s_ffn")
        s_xup = sem("s_xup")
        s_xtr = sem("s_xtr")
        s_xh = sem("s_xh")
        s_xl = sem("s_xl")
        s_v = sem("s_v")
        s_vs = sem("s_vs")
        s_proj = sem("s_proj")
        s_t1 = sem("s_t1")
        s_raw = sem("s_raw")
        s_rot = [sem(f"s_rot{i}") for i in range(2)]
        s_t2 = sem("s_t2")
        s_rope = sem("s_rope")
        s_rh = sem("s_rh")
        s_rl = sem("s_rl")
        s_stack = [sem(f"s_stack{i}") for i in range(4)]
        s_qa = sem("s_qa")
        s_rmax = sem("s_rmax")
        s_max = sem("s_max")
        s_ea = sem("s_ea")
        s_ln = sem("s_ln")
        s_lp = sem("s_lp")
        s_ltr = sem("s_ltr")
        s_lrows = sem("s_lrows")
        s_lse = [sem(f"s_lse{i}") for i in range(GH)]
        s_qb = sem("s_qb")
        s_eb = sem("s_eb")
        s_pv = sem("s_pv")
        s_ch = sem("s_ch")
        s_cl = sem("s_cl")
        s_o = sem("s_o")
        s_oup = sem("s_oup")
        s_out = sem("s_out")

        STORED = 16 * TILES
        block = ctx.enter_context(nc.Block())

        def proj_unit(k, lag=0):
            g, r = divmod(k - lag, STEPS)
            for m in range(4):
                if 0 <= g < GROUPS and PROJ_AT[m] <= r < PROJ_AT[m] + 6:
                    return g, m, r - PROJ_AT[m]

        def proj_after(k, lag):
            u = proj_unit(k, lag)
            return u[:2] if u and u[2] == 5 else None

        def a_tile(k, lag=0):
            g, r = divmod(k - lag, STEPS)
            if 1 <= g <= GROUPS and r < 40 and r % 5 < 4:
                n = r - r // 5
                return g - 1, n // TILES, n % TILES

        def lse_head(k, at):
            g, r = divmod(k - at, STEPS)
            if 1 <= g <= GROUPS and r % 10 == 0 and r < 40:
                return g - 1, r // 10

        def b_unit(k):
            g, r = divmod(k, STEPS)
            if 2 <= g < GROUPS + 2:
                half, j = B_ORDER[r // GH]
                q0 = max(half * HALF, j * P)
                return g - 2, r // GH, r % GH, half, j, q0, (half + 1) * HALF - q0

        def pv_step(k):
            g, r = divmod(k - 6, STEPS)
            if 2 <= g < GROUPS + 2 and r % GH == 0:
                half, j = B_ORDER[r // GH]
                q0 = max(half * HALF, j * P)
                return g - 2, r // GH, half, j, q0, (half + 1) * HALF - q0

        def ctx_half(k):
            s = pv_step(k - 1)
            return (s[0], s[2]) if s and s[3] == 4 * s[2] + 3 else None

        @block.sync
        def _(sp):
            sp.dma_start(wf_s, w_f.rearrange("(a p) o -> p a o", p=P)).then_inc(s_w[4], 16)
            sp.dma_start(ident[:, :], ident_in).then_inc(s_const, 16)
            sp.dma_start(ident16[:, :], ident16_in).then_inc(s_const, 16)
            for i, w in enumerate((w_q, w_k, w_v, w_o)):
                sp.dma_start(stage[i], w.rearrange("(a p) o -> p a o", p=P)).then_inc(s_w[i], 16)
            sp.dma_start(gam[:, :], gamma).then_inc(s_const, 16)
            sp.dma_start(bet[:, :], beta).then_inc(s_const, 16)
            sp.dma_start(biasb[:, :], bias.broadcast_to([P, C])).then_inc(s_const, 16)
            sp.dma_start(cos_s[:, :], cos_t).then_inc(s_const, 16)
            sp.dma_start(sin_s[:, :], sin_t).then_inc(s_const, 16)
            for s in range(SETS):
                for h in range(GH):
                    sp.dma_start(qst[MASK_ROW:LSE_FIRST, s, h, :], q_rows).then_inc(s_rows, 16)
                    sp.dma_start(kst[MASK_ROW:ROWS_B, s, h, :], k_rows).then_inc(s_rows, 16)
            sp.wait_ge(s_tern, 1)
            sp.sem_inc(s_out, 16)
            with sp.Fori(0, BATCH) as b:
                sp.wait_ge(s_out, b * STORED + 16)
                for bl in range(BLOCKS):
                    sp.dma_start(xs[:, 4 * bl:4 * bl + 4, :],
                                 x[bass.ds(b, 1), bl * HALF:(bl + 1) * HALF, :].rearrange("b (t p) c -> p (b t) c", p=P)
                                 ).then_inc(s_x[bl], 16)
                for k in range(LAST_STEP):
                    if u := proj_after(k, 1):
                        n = 4 * u[0] + u[1]
                        sp.wait_ge(s_raw, b * 16 + n + 1)
                        if n >= 2:
                            sp.wait_ge(s_rope, b * 16 + n - 1)
                        for h in range(GH):
                            for a in range(2):
                                o, i = D * h + 16 * a, D * h + 16 * (1 - a)
                                sp.dma_start(rot[o:o + 16, n % 2, :], raw[i:i + 16, n % 2, :]
                                             ).then_inc(s_rot[n % 2], 16)
                    if u := proj_after(k, 8):
                        g, m = u
                        n = 4 * g + m
                        dst, cols = (kst if m % 2 else qst), slice(m // 2 * HALF, (m // 2 + 1) * HALF)
                        parts = (rh, rh, rl) if m % 2 else (rh, rl, rh)
                        sp.wait_ge(s_rh, b * 16 + n + 1)
                        sp.wait_ge(s_rl, b * 16 + n + 1)
                        if g >= SETS:
                            sp.wait_ge(s_qb, b * STEPS * GROUPS + STEPS * (g - SETS + 1))
                        if g >= 1:
                            sp.wait_ge(s_stack[m], (b * GROUPS + g) * 192)
                        for h in range(GH):
                            for a, part in enumerate(parts):
                                sp.dma_start(dst[a * D:(a + 1) * D, g % SETS, h, cols],
                                             part[h * D:(h + 1) * D, n % 2, :]).then_inc(s_stack[m], 16)
                    if e := lse_head(k, 15):
                        g, h = e
                        n = GH * g + h
                        sp.wait_ge(s_lrows, b * 16 + n + 1)
                        for a in range(3):
                            sp.dma_start(qst[LSE_FIRST + a:LSE_FIRST + a + 1, g % SETS, h, :],
                                         lrows[TILES * a:TILES * (a + 1), n % 2, :]
                                         ).then_inc(s_lse[h], 16)
                for r in range(TILES):
                    sp.wait_ge(s_xup, b * 16 + TILES + r + 1)
                    sp.dma_start(out[bass.ds(b, 1), r * P:(r + 1) * P, :].rearrange("b p c -> p (b c)"), xs[:, r, :]).then_inc(s_out, 16)
            sp.wait_ge(s_out, BATCH * STORED + 16)

        @block.gpsimd
        def _(pool):
            pool.memset(ones[:, :], 1.0).then_inc(s_pool0, 1)
            pool.memset(half_neg[:, :], -0.5).then_inc(s_pool0, 1)
            pool.wait_ge(s_pool0, 2)
            pool.wait_ge(s_const, 16 * 7)
            pool.tensor_scalar(biasb[:, :], biasb[:, :], 0.5, None, ALU.mult).then_inc(s_pool0, 1)
            pool.wait_ge(s_pool0, 3)
            links = 0
            with pool.Fori(0, BATCH) as b:

                def rstd_of(bl, i):
                    cols = slice(4 * bl, 4 * bl + 4)
                    pool.wait_ge(s_var, b * 6 + i + 1)
                    pool.tensor_tensor(rstd[:, cols], var_e[:, cols], half_neg[:, cols], ALU.pow).then_inc(s_rstd, 1)

                def add_bias(bl, n):
                    pool.wait_ge(s_y, b * 24 + n)
                    for r in range(4 * bl, 4 * bl + 4):
                        pool.tensor_tensor(xs[:, r, :], xs[:, r, :], biasb[:, :], ALU.add).then_inc(s_xb, 1)

                def low_part(bl, n):
                    for cc in range(CC):
                        pool.wait_ge(s_fh, b * 16 + n + cc + 1)
                        pool.tensor_tensor(fl[:, cc, :], f[:, cc, :], fh[:, cc, :], ALU.subtract).then_inc(s_fl, 1)

                def ffn(i, n_y, n_f):
                    rstd_of(0, i)
                    rstd_of(1, i + 1)
                    add_bias(0, n_y + 4)
                    low_part(0, n_f)
                    add_bias(1, n_y + 8)
                    low_part(1, n_f + 4)

                ffn(0, 0, 0)
                rstd_of(0, 2)
                rstd_of(1, 3)
                for k in range(LAST_STEP):
                    if u := proj_after(k, 3):
                        n = 4 * u[0] + u[1]
                        cols = slice(u[1] // 2 * HALF, (u[1] // 2 + 1) * HALF)
                        pool.wait_ge(s_rot[n % 2], (b * 8 + n // 2 + 1) * 128)
                        pool.tensor_tensor(rot[:, n % 2, :], rot[:, n % 2, :], sin_s[:, cols], ALU.mult).then_inc(s_t2, 1)
                    if u := proj_after(k, 7):
                        n = 4 * u[0] + u[1]
                        pool.wait_ge(s_rh, b * 16 + n + 1)
                        if n >= 2:
                            g2, m2 = divmod(n - 2, 4)
                            pool.wait_ge(s_stack[m2], (b * GROUPS + g2 + 1) * 192)
                        pool.tensor_tensor(rl[:, n % 2, :], t1[:, n % 2, :], rh[:, n % 2, :], ALU.subtract).then_inc(s_rl, 1)
                ffn(4, 16, 8)
                pool.wait_ge(s_out, b * STORED + STORED + 16)

        @block.scalar
        def _(act):
            for i in range(4):
                act.wait_ge(s_w[i], 16)
                nc.scalar.activation(wh[:, i, :, :], stage[i], ACT.Copy, scale=W_SCALE).then_inc(s_wh, 1)
            with act.Fori(0, BATCH) as b:

                def scale_shift(n_t):
                    for cc in range(CC):
                        act.wait_ge(s_ytr, b * 16 + n_t + cc + 1)
                        if n_t + cc >= CC:
                            act.wait_ge(s_fl, b * 16 + n_t + cc + 1 - CC)
                        nc.scalar.activation(f[:, cc, :], tr[cc], ACT.Identity, bias=bet[:, cc:cc + 1],
                                             scale=gam[:, cc:cc + 1]).then_inc(s_f, 1)

                def x_high(bl):
                    for cc in range(CC):
                        act.wait_ge(s_xtr, b * 8 + CC * bl + cc + 1)
                        nc.scalar.activation(xh[:, cc, bl * HALF:(bl + 1) * HALF], tr[cc], ACT.Copy).then_inc(s_xh, 1)

                act.wait_ge(s_const, 16 * 7)
                scale_shift(0)
                scale_shift(CC)
                x_high(0)
                x_high(1)
                for r in range(TILES):
                    act.wait_ge(s_v, b * TILES + r + 1)
                    nc.scalar.activation(vs[:, r, :], ps[2 + r % 2][:, :], ACT.Copy, scale=1.0 / W_SCALE).then_inc(s_vs, 1)
                for k in range(LAST_STEP):
                    if t := b_unit(k):
                        g, st, h, half, j, q0, n = t
                        u = STEPS * g + GH * st + h
                        act.wait_ge(s_qb, b * 192 + u + 1)
                        if 12 * g + st >= 2:
                            act.wait_ge(s_pv, b * 48 + 12 * g + st - 1)
                        nc.scalar.activation(probs[:, st % 2, h, 0:n], pb[u % 2][:, 0:n], ACT.Exp,
                                             scale=EXP_SCALE).then_inc(s_eb, 1)
                    if t := a_tile(k, 1):
                        g, h, i = t
                        a = A_TILES * g + TILES * h + i
                        act.wait_ge(s_max, b * 128 + a + 1)
                        nc.scalar.activation(pa[a % 2][:, 0:(i + 1) * P], pa[a % 2][:, 0:(i + 1) * P], ACT.Exp,
                                             bias=nmax[:, a:a + 1], scale=EXP_SCALE,
                                             accum_out=rsum[:, a:a + 1]).then_inc(s_ea, 1)
                    if e := lse_head(k, 11):
                        n = GH * e[0] + e[1]
                        act.wait_ge(s_ea, b * 128 + TILES * (n + 1))
                        nc.scalar.activation(lsum[:, TILES * n:TILES * (n + 1)], rsum[:, TILES * n:TILES * (n + 1)],
                                             ACT.Ln).then_inc(s_ln, 1)
                    if u := proj_after(k, 1):
                        n = 4 * u[0] + u[1]
                        act.wait_ge(s_t1, b * 16 + n + 1)
                        if n >= 2:
                            act.wait_ge(s_rot[n % 2], (b * 8 + (n - 2) // 2 + 1) * 128)
                        nc.scalar.activation(raw[:, n % 2, :], pp[:, :], ACT.Copy).then_inc(s_raw, 1)
                    if u := proj_after(k, 6):
                        n = 4 * u[0] + u[1]
                        act.wait_ge(s_rope, b * 16 + n + 1)
                        if n >= 2:
                            g2, m2 = divmod(n - 2, 4)
                            act.wait_ge(s_stack[m2], (b * GROUPS + g2 + 1) * 192)
                        nc.scalar.activation(rh[:, n % 2, :], t1[:, n % 2, :], ACT.Copy).then_inc(s_rh, 1)
                    if c := ctx_half(k):
                        g, half = c
                        act.wait_ge(s_pv, b * 48 + 12 * g + 4 + 8 * half)
                        nc.scalar.activation(ch[:, g, half * HALF:(half + 1) * HALF], acc[:, :], ACT.Copy,
                                             scale=CTX_SCALE).then_inc(s_ch, 1)
                scale_shift(2 * CC)
                scale_shift(3 * CC)
                act.wait_ge(s_out, b * STORED + STORED + 16)

        @block.vector
        def _(dve):
            dve.wait_ge(s_w[4], 16)
            nc.vector.tensor_reduce(sums[:, 0:1], wf_s, AX.XY, ALU.add, apply_absolute_value=True).then_inc(s_abs, 1)
            dve.wait_ge(s_tot, 1)
            nc.vector.tensor_scalar(sums[:, 1:2], ps[3][:, 0:1], 1.0 / (C * C), Q_EPS, ALU.mult, ALU.add).then_inc(s_abs, 1)
            dve.wait_ge(s_abs, 2)
            nc.vector.tensor_scalar(sums[:, 2:3], sums[:, 1:2], 0.5, None, ALU.mult).then_inc(s_abs, 1)
            nc.vector.tensor_scalar(sums[:, 3:4], sums[:, 1:2], -0.5, None, ALU.mult).then_inc(s_abs, 1)
            dve.wait_ge(s_abs, 4)
            nc.vector.tensor_scalar(wtg, wf_s, sums[:, 2:3], None, ALU.is_gt).then_inc(s_abs, 1)
            dve.wait_ge(s_abs, 5)
            nc.vector.scalar_tensor_tensor(wt[:, :, :], wf_s, sums[:, 3:4], wtg, ALU.is_lt, ALU.subtract).then_inc(s_tern, 1)
            for i in range(4):
                dve.wait_ge(s_wh, i + 1)
                nc.vector.scalar_tensor_tensor(wl[:, i, :, :], stage[i], W_SCALE, wh[:, i, :, :],
                                               ALU.mult, ALU.subtract).then_inc(s_wl, 1)
            with dve.Fori(0, BATCH) as b:
                links = [0]

                def link(ins):
                    links[0] += 1
                    ins.then_inc(s_link, 1)
                    dve.wait_ge(s_link, b * DVE_LINKS + links[0])

                def statistics(bl, n, mul, add):
                    for r in range(4 * bl, 4 * bl + 4):
                        last = nc.vector.bn_stats(stats[:, r, :], xs[:, r, :])
                        last = last.then_inc(s_link, 1)
                        links[0] += 1
                    dve.wait_ge(s_link, b * DVE_LINKS + links[0])
                    nc.vector.memset(hold[:, n - 1:n], 0.0)
                    for r in range(4 * bl, 4 * bl + 4):
                        nc.vector.bn_aggr(mv[:, r, :], stats[:, r, :]).then_inc(s_aggr, 1)
                    dve.wait_ge(s_aggr, b * 24 + 4 * n)
                    cols = slice(4 * bl, 4 * bl + 4)
                    nc.vector.tensor_scalar(var_e[:, cols], mv[:, cols, 1], mul, add, ALU.mult, ALU.add).then_inc(s_var, 1)

                def normalize(bl, n, n_tr):
                    dve.wait_ge(s_rstd, b * 6 + n)
                    if n_tr:
                        dve.wait_ge(*n_tr)
                    for r in range(4 * bl, 4 * bl + 4):
                        nc.vector.tensor_scalar(y[:, bl, r % 4, :], xs[:, r, :], mv[:, r, 0:1], rstd[:, r:r + 1],
                                                ALU.subtract, ALU.mult).then_inc(s_y, 1)

                def f_high(n):
                    for cc in range(CC):
                        dve.wait_ge(s_f, b * 16 + n + cc + 1)
                        if n + cc >= CC:
                            dve.wait_ge(s_ffn, b * 16 + n)
                        nc.vector.tensor_copy(fh[:, cc, :], f[:, cc, :]).then_inc(s_fh, 1)

                def ffn_update(bl, n):
                    for i, r in enumerate(range(4 * bl, 4 * bl + 4)):
                        dve.wait_ge(s_ffn, b * 16 + n + i + 1)
                        dve.wait_ge(s_xb, b * 16 + n + i + 1)
                        nc.vector.scalar_tensor_tensor(xs[:, r, :], ps[r % 2][:, :], -0.5, xs[:, r, :],
                                                       ALU.mult, ALU.add).then_inc(s_xup, 1)

                def ffn(n_r, n_f, y_free):
                    statistics(0, n_r + 1, 1 + LN_EPS, LN_EPS * LN_EPS)
                    statistics(1, n_r + 2, 1 + LN_EPS, LN_EPS * LN_EPS)
                    normalize(0, n_r + 1, y_free)
                    normalize(1, n_r + 2, None)
                    f_high(n_f)
                    ffn_update(0, n_f)
                    f_high(n_f + 4)
                    ffn_update(1, n_f + 4)

                dve.wait_ge(s_x[0], b * 16 + 16)
                dve.wait_ge(s_x[1], b * 16 + 16)
                ffn(0, 0, None)
                for bl in range(BLOCKS):
                    dve.wait_ge(s_xup, b * 16 + 4 * bl + 4)
                    statistics(bl, 3 + bl, 1.0, LN_EPS)
                    normalize(bl, 3 + bl, (s_ytr, b * 16 + 4 * bl + 4))
                for bl in range(BLOCKS):
                    for cc in range(CC):
                        n = CC * bl + cc
                        dve.wait_ge(s_xh, b * 8 + n + 1)
                        cols = slice(bl * HALF, (bl + 1) * HALF)
                        nc.vector.tensor_tensor(xl[:, cc, cols], tr[cc], xh[:, cc, cols], ALU.subtract).then_inc(s_xl, 1)
                for k in range(LAST_STEP):
                    if t := a_tile(k):
                        g, h, i = t
                        a = A_TILES * g + TILES * h + i
                        dve.wait_ge(s_qa, b * 128 + a + 1)
                        nc.vector.tensor_reduce(rmax[:, a:a + 1], pa[a % 2][:, 0:(i + 1) * P], AX.X, ALU.max,
                                                negate=True).then_inc(s_rmax, 1)
                        dve.wait_ge(s_rmax, b * 128 + a + 1)
                        nc.vector.tensor_scalar(nmax[:, a:a + 1], rmax[:, a:a + 1], EXP_SCALE, None,
                                                ALU.mult).then_inc(s_max, 1)
                    if u := proj_after(k, 1):
                        n = 4 * u[0] + u[1]
                        cols = slice(u[1] // 2 * HALF, (u[1] // 2 + 1) * HALF)
                        dve.wait_ge(s_proj, b * 16 + n + 1)
                        if n >= 2:
                            dve.wait_ge(s_rl, b * 16 + n - 1)
                        nc.vector.tensor_tensor(t1[:, n % 2, :], pp[:, :], cos_s[:, cols], ALU.mult).then_inc(s_t1, 1)
                    if u := proj_after(k, 5):
                        n = 4 * u[0] + u[1]
                        dve.wait_ge(s_t2, b * 16 + n + 1)
                        dve.wait_ge(s_t1, b * 16 + n + 1)
                        nc.vector.tensor_tensor(t1[:, n % 2, :], t1[:, n % 2, :], rot[:, n % 2, :], ALU.add).then_inc(s_rope, 1)
                    if e := lse_head(k, 12):
                        n = GH * e[0] + e[1]
                        s = n % 2
                        cols = slice(TILES * n, TILES * (n + 1))
                        dve.wait_ge(s_ln, b * 16 + n + 1)
                        if n >= 2:
                            dve.wait_ge(s_ltr, b * 16 + n - 1)
                        link(nc.vector.tensor_tensor(lrow[:, s, :], nmax[:, cols], lsum[:, cols], ALU.subtract))
                        link(nc.vector.tensor_scalar(lrow[:, s, :], lrow[:, s, :], 1.0 / (EXP_SCALE * LSE_ROW), None, ALU.mult))
                        link(nc.vector.tensor_copy(lparts[:, s, 0, :], lrow[:, s, :]))
                        link(nc.vector.tensor_tensor(lres[:, s, :], lrow[:, s, :], lparts[:, s, 0, :], ALU.subtract))
                        link(nc.vector.tensor_copy(lparts[:, s, 1, :], lres[:, s, :]))
                        nc.vector.tensor_tensor(lparts[:, s, 2, :], lres[:, s, :], lparts[:, s, 1, :],
                                                ALU.subtract).then_inc(s_lp, 1)
                    if e := lse_head(k, 15):
                        n = GH * e[0] + e[1]
                        dve.wait_ge(s_ltr, b * 16 + n + 1)
                        if n >= 2:
                            g2, h2 = divmod(n - 2, GH)
                            dve.wait_ge(s_lse[h2], (b * GROUPS + g2 + 1) * 48)
                        nc.vector.tensor_copy(lrows[:, n % 2, :], pp[0:3 * TILES, 0:P // 2].bitcast(F16)).then_inc(s_lrows, 1)
                    if c := ctx_half(k):
                        g, half = c
                        cols = slice(half * HALF, (half + 1) * HALF)
                        dve.wait_ge(s_ch, b * 8 + 2 * g + half + 1)
                        nc.vector.scalar_tensor_tensor(cl[:, g, cols], acc[:, :], CTX_SCALE, ch[:, g, cols],
                                                       ALU.mult, ALU.subtract).then_inc(s_cl, 1)
                for r in range(TILES):
                    dve.wait_ge(s_o, b * TILES + r + 1)
                    nc.vector.scalar_tensor_tensor(xs[:, r, :], ps[2 + r % 2][:, :], 1.0 / (CTX_SCALE * W_SCALE),
                                                   xs[:, r, :], ALU.mult, ALU.add).then_inc(s_oup, 1)
                dve.wait_ge(s_oup, b * TILES + TILES)
                ffn(4, 8, None)
                assert links[0] == DVE_LINKS, links
                dve.wait_ge(s_out, b * STORED + STORED + 16)

        @block.tensor
        def _(pe):
            pe.wait_ge(s_pool0, 1)
            pe.wait_ge(s_abs, 1)
            nc.tensor.matmul(ps[3][:, 0:1], ones[:, :], sums[:, 0:1], start=True, stop=True).then_inc(s_tot, 1)
            pe.wait_ge(s_const, 16 * 7)
            pe.wait_ge(s_tern, 1)
            pe.wait_ge(s_wl, 4)
            pe.wait_ge(s_rows, 16 * 2 * SETS * GH)
            with pe.Fori(0, BATCH) as b:

                def y_chunks(bl, s_done):
                    for cc in range(CC):
                        for r in range(4):
                            last = nc.tensor.transpose(tr[cc][:, r * P:(r + 1) * P], y[:, bl, r, cc * P:(cc + 1) * P],
                                                       ident[:, :])
                        last.then_inc(s_done, 1)

                def ffn_products(bl, n):
                    pe.wait_ge(s_fh, b * 16 + n + CC)
                    pe.wait_ge(s_fl, b * 16 + n + CC)
                    for i in range(4):
                        if n + i >= 2:
                            pe.wait_ge(s_xup, b * 16 + n + i - 1)
                        for a, part in enumerate((fh, fl)):
                            for cc in range(CC):
                                last = nc.tensor.matmul(ps[i % 2][:, :], part[:, cc, i * P:(i + 1) * P], wt[:, cc, :],
                                                        start=(a == 0 and cc == 0), stop=(a == 1 and cc == CC - 1))
                        last.then_inc(s_ffn, 1)

                def ffn(n_y, n_f):
                    pe.wait_ge(s_y, b * 24 + n_y + 4)
                    y_chunks(0, s_ytr)
                    pe.wait_ge(s_y, b * 24 + n_y + 8)
                    pe.wait_ge(s_f, b * 16 + n_f + 4)
                    y_chunks(1, s_ytr)
                    ffn_products(0, n_f)
                    ffn_products(1, n_f + 4)

                ffn(0, 0)
                for bl in range(BLOCKS):
                    pe.wait_ge(s_y, b * 24 + 12 + 4 * bl)
                    if bl:
                        pe.wait_ge(s_xl, b * 8 + 4)
                    else:
                        pe.wait_ge(s_f, b * 16 + 8)
                    y_chunks(bl, s_xtr)

                def products(dst, lhs, rhs, order):
                    for n, (a, c) in enumerate(order):
                        last = nc.tensor.matmul(dst, lhs(a, c), rhs(a, c), start=(n == 0), stop=(n == len(order) - 1))
                    return last

                PASSES = [(0, 0), (1, 0), (0, 1)]
                xp, cp, wp = (xh, xl), (ch, cl), (wh, wl)
                for r in range(TILES):
                    pe.wait_ge(s_xl, b * 8 + 4 * (r // 4) + 4)
                    if r >= 2:
                        pe.wait_ge(s_vs, b * TILES + r - 1)
                    n = 0
                    for pa_, pb_ in PASSES:
                        for cc in range(CC):
                            last = nc.tensor.matmul(ps[2 + r % 2][:, :], xp[pa_][:, cc, r * P:(r + 1) * P],
                                                    wp[pb_][:, 2, cc, :], start=(n == 0), stop=(n == 3 * CC - 1))
                            n += 1
                    last.then_inc(s_v, 1)
                pe.wait_ge(s_vs, b * TILES + TILES)
                evacuated = 0
                transposed = 0
                for k in range(LAST_STEP):
                    if t := b_unit(k):
                        g, st, h, half, j, q0, n = t
                        u = STEPS * g + GH * st + h
                        if st == 0 or st == 4:
                            pe.wait_ge(s_lse[h], (b * GROUPS + g + 1) * 48)
                        if u >= 2:
                            pe.wait_ge(s_eb, b * 192 + u - 1)
                        nc.tensor.matmul(pb[u % 2][:, 0:n], kst[0:ROWS_B, g % SETS, h, j * P:(j + 1) * P],
                                         qst[0:ROWS_B, g % SETS, h, q0:q0 + n], start=True, stop=True).then_inc(s_qb, 1)
                    if t := a_tile(k):
                        g, h, i = t
                        a = A_TILES * g + TILES * h + i
                        if h == 0:
                            for m in range(2 + 2 * (i // 4)):
                                pe.wait_ge(s_stack[m], (b * GROUPS + g + 1) * 192)
                        if a >= 2:
                            pe.wait_ge(s_ea, b * 128 + a - 1)
                        for c0 in range(0, (i + 1) * P, HALF):
                            n = min(HALF, (i + 1) * P - c0)
                            last = nc.tensor.matmul(pa[a % 2][:, c0:c0 + n], qst[0:ROWS_A, g % SETS, h, i * P:(i + 1) * P],
                                                    kst[0:ROWS_A, g % SETS, h, c0:c0 + n], start=True, stop=True)
                        last.then_inc(s_qa, 1)
                    if u := proj_unit(k):
                        g, m, i = u
                        if i == 0:
                            if evacuated:
                                pe.wait_ge(s_raw, b * 16 + evacuated)
                            if transposed:
                                pe.wait_ge(s_lrows, b * 16 + transposed)
                        for n in (2 * i, 2 * i + 1):
                            a, cc = divmod(n, CC)
                            xw, ww = ((0, 0), (1, 0), (0, 1))[a]
                            last = nc.tensor.matmul(pp[:, :], wp[ww][:, m % 2, cc, g * P:(g + 1) * P],
                                                    xp[xw][:, cc, m // 2 * HALF:(m // 2 + 1) * HALF],
                                                    start=(n == 0), stop=(n == 3 * CC - 1))
                        if i == 5:
                            last.then_inc(s_proj, 1)
                            evacuated += 1
                    if e := lse_head(k, 14):
                        n = GH * e[0] + e[1]
                        if evacuated:
                            pe.wait_ge(s_raw, b * 16 + evacuated)
                        pe.wait_ge(s_lp, b * 16 + n + 1)
                        if transposed:
                            pe.wait_ge(s_lrows, b * 16 + transposed)
                        nc.tensor.transpose(pp[0:3 * TILES, 0:P // 2].bitcast(F16),
                                            lparts[:, n % 2, :, :].rearrange("p a t -> p (a t)"),
                                            ident16[:, :]).then_inc(s_ltr, 1)
                        transposed += 1
                    if t := pv_step(k):
                        g, st, half, j, q0, n = t
                        pe.wait_ge(s_eb, b * 192 + STEPS * g + GH * (st + 1))
                        if j == 0 and (g or half):
                            pe.wait_ge(s_cl, b * 8 + 2 * g + half)
                        for h in range(GH):
                            last = nc.tensor.matmul(acc[h * D:(h + 1) * D, q0 - half * HALF:HALF],
                                                    vs[:, j, (GH * g + h) * D:(GH * g + h + 1) * D],
                                                    probs[:, st % 2, h, 0:n], start=(j == 0), stop=(j == 4 * half + 3),
                                                    skip_group_check=True)
                        last.then_inc(s_pv, 1)
                pe.wait_ge(s_lrows, b * 16 + 16)
                pe.wait_ge(s_cl, b * 8 + 8)
                for r in range(TILES):
                    if r >= 2:
                        pe.wait_ge(s_oup, b * TILES + r - 1)
                    n = 0
                    for pa_, pb_ in PASSES:
                        for g in range(GROUPS):
                            last = nc.tensor.matmul(ps[2 + r % 2][:, :], cp[pa_][:, g, r * P:(r + 1) * P],
                                                    wp[pb_][:, 3, g, :], start=(n == 0), stop=(n == 3 * GROUPS - 1))
                            n += 1
                    last.then_inc(s_o, 1)
                ffn(16, 8)
                pe.wait_ge(s_out, b * STORED + STORED + 16)


_INS = ["L0_attn_x", "L0_attn_w_q", "L0_attn_w_k", "L0_attn_w_v", "L0_attn_w_o", "L0_ffn_weight",
        "L0_ffn_bias", "L0_ffn_ln_gamma", "L0_ffn_ln_beta"]


def _constants():
    import numpy as np
    inv = (np.float32(1.0) / np.power(np.float32(10000.0), np.arange(0, D, 2, dtype=np.float32) / np.float32(D))).astype(np.float32)
    freqs = np.outer(np.arange(T, dtype=np.float32), inv).astype(np.float32)
    unit = QK_SCALE / W_SCALE
    dim = np.arange(P) % D
    cos = (np.cos(freqs).astype(np.float32)[:, dim % 16].T * np.float32(unit)).astype(np.float32)
    sign = np.where(dim < 16, -1.0, 1.0).astype(np.float32)[:, None]
    sin = (np.sin(freqs).astype(np.float32)[:, dim % 16].T * sign * np.float32(unit)).astype(np.float32)
    tok = np.arange(T)
    own = np.arange(TILES)[:, None] == tok[None, :] // P
    late = (tok % P >= 64)[None, :]
    q_rows = np.where(own & ~late, 32768.0, 0.0).astype(np.float16)
    k_rows = np.concatenate([np.where(own & late, -32768.0, 0.0), np.full((3, T), LSE_ROW)]).astype(np.float16)
    return {"cos_t": np.ascontiguousarray(cos), "sin_t": np.ascontiguousarray(sin),
            "ident": np.eye(P, dtype=np.float32), "ident16": np.eye(P, dtype=np.float16),
            "q_rows": q_rows, "k_rows": k_rows}


def kernel(**inputs):
    import numpy as _np
    import concourse.bacc as _bacc
    from concourse import mybir as _mybir
    from concourse.bass_utils import run_bass_kernel_spmd as _run

    nc = _bacc.Bacc("TRN2", target_bir_lowering=False, num_devices=1)
    arrays, args = {}, []
    named = [(n, _np.asarray(inputs[n])) for n in _INS]
    named = [(n, _np.ascontiguousarray(a.T if "_w" in n else a.reshape(CC, P).T if "_ln_" in n else a.reshape(1, C)
                                       if "_bias" in n else a)) for n, a in named] + list(_constants().items())
    for name, a in named:
        arrays[f"in_{name}_dram"] = a
        args.append(nc.dram_tensor(f"in_{name}_dram", a.shape, _mybir.dt.from_np(a.dtype), kind="ExternalInput").ap())
    out = nc.dram_tensor("out_0_dram", (BATCH, T, C), F32, kind="ExternalOutput").ap()
    macaron(nc, *args, out)
    r = _run(nc, [arrays], core_ids=[0])
    return r.results[0]["out_0_dram"]
```

```python
from contextlib import ExitStack

import concourse.bass as bass
from concourse import mybir

F32 = mybir.dt.float32
F16 = mybir.dt.float16
ALU = mybir.AluOpType
ACT = mybir.ActivationFunctionType
AX = mybir.AxisListType

BATCH, T, C, HEADS = 2, 1024, 512, 16
D = C // HEADS
P = 128
TILES = T // P
CC = C // P
HALF = 512
BLOCKS = T // HALF
GH = P // D
GROUPS = HEADS // GH
SETS = 3
LN_EPS = 1e-5
Q_EPS = 1e-5
W_SCALE = 64.0
QK_SCALE = 16.0
CTX_SCALE = 16.0
EXP_SCALE = float(D) ** -0.5 / (QK_SCALE * QK_SCALE)
MAX_SCALE = 2048.0
MASK_ROW = 3 * D
MAX_ROW = MASK_ROW + TILES
ROWS_A = MAX_ROW
ROWS_B = MAX_ROW + 2

STEPS = 48
A_START, B_START = 8, 16
A_ORDER = [(i, half) for i in range(TILES) for half in range(i // 4 + 1)]
A_UNITS = len(A_ORDER)
B_ORDER = [(half, j) for half in range(BLOCKS) for j in range(4 * half + 4)]
LAST_STEP = STEPS * (GROUPS + 2) + B_START + 8
DVE_LINKS = 3 * TILES + 2 * HEADS


def macaron(nc, x, w_q, w_k, w_v, w_o, w_f, bias, gamma, beta, cos_t, sin_t, ident_in, ident16_in,
            q_rows, k_rows, spread, out):
    ctx = ExitStack()
    with ctx:
        def sb(name, shape, dt):
            return ctx.enter_context(nc.sbuf_tensor(name, shape, dt))

        def sem(name):
            return ctx.enter_context(nc.semaphore(name))

        xs = sb("xs", [P, TILES, C], F32)
        xh = sb("xh", [P, CC, T], F16)
        xl = sb("xl", [P, CC, T], F16)
        vs = sb("vs", [P, TILES, C], F32)
        ch = sb("ch", [P, GROUPS, T], F16)
        cl = sb("cl", [P, GROUPS, T], F16)
        wh = sb("wh", [P, 4, CC, C], F16)
        wl = sb("wl", [P, 4, CC, C], F16)
        wt = sb("wt", [P, CC, C], F16)
        cos_s = sb("cos_s", [P, T], F32)
        sin_s = sb("sin_s", [P, T], F32)
        qst = sb("qst", [P, SETS, GH, T], F16)
        kst = sb("kst", [P, SETS, GH, T], F16)
        rhl = sb("rhl", [P, 2, 2, HALF], F16)
        t1 = sb("t1", [P, 2, HALF], F32)
        fh = sb("fh", [P, CC, HALF], F16)
        fl = sb("fl", [P, CC, HALF], F16)
        big = sb("big", [P, 24 * 256], F32)
        y = big[:, 0:4096].rearrange("p (b t c) -> p b t c", b=2, t=4)
        f = big[:, 4096:6144].rearrange("p (c n) -> p c n", c=CC)
        probs = big[:, 0:4096].rearrange("p (s h n) -> p s h n", s=2, h=GH)
        rot = big[:, 4096:5120].rearrange("p (s n) -> p s n", s=2)
        rec = big[:, 5120:5632]
        cf = big[:, 5632:6144]
        stage = [vs[:, 0:4, :], vs[:, 4:8, :],
                 ch[:, :, :].rearrange("p g t -> p (g t)").bitcast(F32).rearrange("p (a b) -> p a b", a=4),
                 cl[:, :, :].rearrange("p g t -> p (g t)").bitcast(F32).rearrange("p (a b) -> p a b", a=4)]
        wf_s = xs[:, 0:4, :]
        wtg = xl[:, 0:2, :].rearrange("p a t -> p (a t)").rearrange("p (a b) -> p a b", a=4)
        biasb = sb("biasb", [P, C], F32)
        ident = sb("ident", [P, P], F32)
        ident16 = sb("ident16", [P, P], F16)
        ones = sb("ones", [P, P], F32)
        gam = sb("gam", [P, CC], F32)
        bet = sb("bet", [P, CC], F32)
        sums = sb("sums", [P, 4], F32)
        stats = sb("stats", [P, TILES, 6], F32)
        mv = sb("mv", [P, TILES, 2], F32)
        var_e = sb("var_e", [P, TILES], F32)
        half_neg = sb("half_neg", [P, TILES], F32)
        rstd = sb("rstd", [P, TILES], F32)
        rmax = sb("rmax", [P, HEADS * A_UNITS], F32)
        mparts = sb("mparts", [P, 2, 2, TILES], F16)
        mrows = sb("mrows", [2 * TILES, 2, P], F16)
        hold = sb("hold", [P, 6], F32)

        bank = [ctx.enter_context(nc.psum_tensor(f"bank{i}", [P, HALF], F32)) for i in range(8)]
        pa = bank[0:3]
        pb = bank[3:5]
        acc = bank[5]
        psum = bank[6]
        pp = bank[7]
        tr = [t[:, :] for t in bank[0:4]]
        pf = [bank[4], bank[6]]
        pw = [bank[5], bank[7]]

        s_const = sem("s_const")
        s_w = [sem(f"s_w{i}") for i in range(5)]
        s_rows = sem("s_rows")
        s_pool0 = sem("s_pool0")
        s_abs = sem("s_abs")
        s_tot = sem("s_tot")
        s_tern = sem("s_tern")
        s_wh = sem("s_wh")
        s_wl = sem("s_wl")
        s_x = [sem(f"s_x{i}") for i in range(BLOCKS)]
        s_link = sem("s_link")
        s_aggr = sem("s_aggr")
        s_var = sem("s_var")
        s_rstd = sem("s_rstd")
        s_y = sem("s_y")
        s_xb = sem("s_xb")
        s_ytr = sem("s_ytr")
        s_f = sem("s_f")
        s_fh = sem("s_fh")
        s_fl = sem("s_fl")
        s_ffn = sem("s_ffn")
        s_xup = sem("s_xup")
        s_xtr = sem("s_xtr")
        s_xh = sem("s_xh")
        s_xl = sem("s_xl")
        s_v = sem("s_v")
        s_vs = sem("s_vs")
        s_proj = sem("s_proj")
        s_rot = sem("s_rot")
        s_spread = [sem(f"s_spread{i}") for i in range(2)]
        s_rope = sem("s_rope")
        s_rh = sem("s_rh")
        s_rl = sem("s_rl")
        s_stack = [sem(f"s_stack{i}") for i in range(4)]
        s_qa = sem("s_qa")
        s_max = sem("s_max")
        s_mp = sem("s_mp")
        s_mtr = sem("s_mtr")
        s_mrows = sem("s_mrows")
        s_mdma = [sem(f"s_mdma{i}") for i in range(GH)]
        s_qb = sem("s_qb")
        s_eb = sem("s_eb")
        s_pv = sem("s_pv")
        s_ln = sem("s_ln")
        s_rec = sem("s_rec")
        s_cf = sem("s_cf")
        s_ch = sem("s_ch")
        s_cl = sem("s_cl")
        s_o = sem("s_o")
        s_oup = sem("s_oup")
        s_out = sem("s_out")

        STORED = 16 * TILES
        block = ctx.enter_context(nc.Block())

        def proj_unit(k, lag=0):
            g, r = divmod(k - lag, STEPS)
            if 0 <= g < GROUPS and r % A_UNITS < 6:
                return g, r // A_UNITS, r % A_UNITS

        def proj_after(k, lag):
            u = proj_unit(k, lag)
            return u[:2] if u and u[2] == 5 else None

        def a_unit(k):
            g, r = divmod(k - A_START, STEPS)
            if 1 <= g <= GROUPS:
                return g - 1, r // A_UNITS, *A_ORDER[r % A_UNITS]

        def max_head(k, lag):
            t = a_unit(k - lag)
            return t[:2] if t and t[2:] == A_ORDER[-1] else None

        def b_unit(k):
            g, r = divmod(k - B_START, STEPS)
            if 2 <= g < GROUPS + 2:
                half, j = B_ORDER[r // GH]
                q0 = max(half * HALF, j * P)
                return g - 2, r // GH, r % GH, half, j, q0, (half + 1) * HALF - q0

        def pv_step(k):
            t = b_unit(k - 6)
            return (t[0], t[1], *t[3:]) if t and t[2] == 0 else None

        def ctx_half(k, lag=1):
            s = pv_step(k - lag)
            return (s[0], s[2]) if s and s[3] == 4 * s[2] + 3 else None

        @block.sync
        def _(sp):
            sp.dma_start(wf_s, w_f.rearrange("(a p) o -> p a o", p=P)).then_inc(s_w[4], 16)
            sp.dma_start(ident[:, :], ident_in).then_inc(s_const, 16)
            sp.dma_start(ident16[:, :], ident16_in).then_inc(s_const, 16)
            for i, w in enumerate((w_q, w_k, w_v, w_o)):
                sp.dma_start(stage[i], w.rearrange("(a p) o -> p a o", p=P)).then_inc(s_w[i], 16)
            sp.dma_start(gam[:, :], gamma).then_inc(s_const, 16)
            sp.dma_start(bet[:, :], beta).then_inc(s_const, 16)
            sp.dma_start(biasb[:, :], bias.broadcast_to([P, C])).then_inc(s_const, 16)
            sp.dma_start(cos_s[:, :], cos_t).then_inc(s_const, 16)
            sp.dma_start(sin_s[:, :], sin_t).then_inc(s_const, 16)
            for stack, first, last, rows in ((qst, MASK_ROW, MAX_ROW, q_rows), (kst, MASK_ROW, ROWS_B, k_rows)):
                sp.dma_start(stack[first:last, :, :, :].rearrange("r s h t -> r (s h) t"),
                             rows.rearrange("r (a t) -> r a t", a=1).broadcast_to([last - first, SETS * GH, T])
                             ).then_inc(s_rows, 16)
            sp.wait_ge(s_tern, 1)
            sp.sem_inc(s_out, 16)
            with sp.Fori(0, BATCH) as b:
                sp.wait_ge(s_out, b * STORED + 16)
                for bl in range(BLOCKS):
                    sp.dma_start(xs[:, 4 * bl:4 * bl + 4, :],
                                 x[bass.ds(b, 1), bl * HALF:(bl + 1) * HALF, :].rearrange("b (t p) c -> p (b t) c", p=P)
                                 ).then_inc(s_x[bl], 16)
                for k in range(LAST_STEP):
                    if u := proj_after(k, 6):
                        g, m = u
                        n = 4 * g + m
                        sp.wait_ge(s_rl, b * 16 + n + 1)
                        if n >= 2:
                            g2, m2 = divmod(n - 2, 4)
                            sp.wait_ge(s_stack[m2], (b * GROUPS + g2 + 1) * 16)
                        low, again = (slice(0, 3, 2), 1) if m % 2 else (slice(0, 2), 2)
                        sp.dma_start(spread[n % 2, low].rearrange("a p t -> p a t"), rhl[:, n % 2, :, :]
                                     ).then_inc(s_spread[n % 2], 16)
                        sp.dma_start(spread[n % 2, again], rhl[:, n % 2, 0, :]).then_inc(s_spread[n % 2], 16)
                    if u := proj_after(k, 9):
                        g, m = u
                        n = 4 * g + m
                        dst, cols = (kst if m % 2 else qst), slice(m // 2 * HALF, (m // 2 + 1) * HALF)
                        sp.wait_ge(s_spread[n % 2], (b * 8 + n // 2 + 1) * 32)
                        if g >= SETS:
                            sp.wait_ge(s_qb, b * STEPS * GROUPS + STEPS * (g - SETS + 1))
                        sp.dma_start(dst[0:MASK_ROW, g % SETS, :, cols],
                                     spread[n % 2].rearrange("a (d h) t -> (a d) h t", h=GH)).then_inc(s_stack[m], 16)
                    if e := max_head(k, 5):
                        g, h = e
                        n = GH * g + h
                        sp.wait_ge(s_mrows, b * 16 + n + 1)
                        sp.dma_start(qst[MAX_ROW:ROWS_B, g % SETS, h, :], mrows[:, n % 2, :]).then_inc(s_mdma[h], 16)
                for r in range(TILES):
                    sp.wait_ge(s_xup, b * 16 + TILES + r + 1)
                    sp.dma_start(out[bass.ds(b, 1), r * P:(r + 1) * P, :].rearrange("b p c -> p (b c)"), xs[:, r, :]).then_inc(s_out, 16)
            sp.wait_ge(s_out, BATCH * STORED + 16)

        @block.gpsimd
        def _(pool):
            pool.memset(ones[:, :], 1.0).then_inc(s_pool0, 1)
            pool.memset(half_neg[:, :], -0.5).then_inc(s_pool0, 1)
            pool.wait_ge(s_pool0, 2)
            pool.wait_ge(s_const, 16 * 7)
            pool.tensor_scalar(biasb[:, :], biasb[:, :], 0.5, None, ALU.mult).then_inc(s_pool0, 1)
            pool.wait_ge(s_pool0, 3)
            links = 0
            with pool.Fori(0, BATCH) as b:

                def rstd_of(bl, i):
                    cols = slice(4 * bl, 4 * bl + 4)
                    pool.wait_ge(s_var, b * 6 + i + 1)
                    pool.tensor_tensor(rstd[:, cols], var_e[:, cols], half_neg[:, cols], ALU.pow).then_inc(s_rstd, 1)

                def add_bias(bl, n):
                    pool.wait_ge(s_y, b * 24 + n)
                    for r in range(4 * bl, 4 * bl + 4):
                        pool.tensor_tensor(xs[:, r, :], xs[:, r, :], biasb[:, :], ALU.add).then_inc(s_xb, 1)

                def low_part(bl, n):
                    for cc in range(CC):
                        pool.wait_ge(s_fh, b * 16 + n + cc + 1)
                        pool.tensor_tensor(fl[:, cc, :], f[:, cc, :], fh[:, cc, :], ALU.subtract).then_inc(s_fl, 1)

                def ffn(i, n_y, n_f):
                    rstd_of(0, i)
                    rstd_of(1, i + 1)
                    add_bias(0, n_y + 4)
                    low_part(0, n_f)
                    add_bias(1, n_y + 8)
                    low_part(1, n_f + 4)

                ffn(0, 0, 0)
                rstd_of(0, 2)
                rstd_of(1, 3)
                for k in range(LAST_STEP):
                    if u := proj_after(k, 2):
                        n = 4 * u[0] + u[1]
                        pool.wait_ge(s_rot, b * 16 + n + 1)
                        pool.tensor_tensor(t1[:, n % 2, :], t1[:, n % 2, :], rot[:, n % 2, :], ALU.add).then_inc(s_rope, 1)
                    if u := proj_after(k, 5):
                        n = 4 * u[0] + u[1]
                        pool.wait_ge(s_rh, b * 16 + n + 1)
                        pool.tensor_tensor(rhl[:, n % 2, 1, :], t1[:, n % 2, :], rhl[:, n % 2, 0, :], ALU.subtract
                                           ).then_inc(s_rl, 1)
                    if c := ctx_half(k, 5):
                        g, half = c
                        cols = slice(half * HALF, (half + 1) * HALF)
                        pool.wait_ge(s_ch, b * 8 + 2 * g + half + 1)
                        pool.tensor_tensor(cl[:, g, cols], cf, ch[:, g, cols], ALU.subtract).then_inc(s_cl, 1)
                ffn(4, 16, 8)
                pool.wait_ge(s_out, b * STORED + STORED + 16)

        @block.scalar
        def _(act):
            nc.scalar.preload_act_table_set("natural_log_exp_and_others")
            for i in range(4):
                act.wait_ge(s_w[i], 16)
                nc.scalar.activation(wh[:, i, :, :], stage[i], ACT.Copy, scale=W_SCALE).then_inc(s_wh, 1)
            with act.Fori(0, BATCH) as b:

                def scale_shift(n_t):
                    for cc in range(CC):
                        act.wait_ge(s_ytr, b * 16 + n_t + cc + 1)
                        if n_t + cc >= CC:
                            act.wait_ge(s_fl, b * 16 + n_t + cc + 1 - CC)
                        nc.scalar.activation(f[:, cc, :], tr[cc], ACT.Identity, bias=bet[:, cc:cc + 1],
                                             scale=gam[:, cc:cc + 1]).then_inc(s_f, 1)

                def x_high(bl):
                    for cc in range(CC):
                        act.wait_ge(s_xtr, b * 8 + CC * bl + cc + 1)
                        nc.scalar.activation(xh[:, cc, bl * HALF:(bl + 1) * HALF], tr[cc], ACT.Copy).then_inc(s_xh, 1)

                act.wait_ge(s_const, 16 * 7)
                scale_shift(0)
                scale_shift(CC)
                x_high(0)
                x_high(1)
                for r in range(TILES):
                    act.wait_ge(s_v, b * TILES + r + 1)
                    nc.scalar.activation(vs[:, r, :], pw[r % 2][:, :], ACT.Copy, scale=1.0 / W_SCALE).then_inc(s_vs, 1)
                for k in range(LAST_STEP):
                    if t := b_unit(k):
                        g, st, h, half, j, q0, n = t
                        u = STEPS * g + GH * st + h
                        act.wait_ge(s_qb, b * 192 + u + 1)
                        if 12 * g + st >= 2:
                            act.wait_ge(s_pv, b * 48 + 12 * g + st - 1)
                        nc.scalar.activation(probs[:, st % 2, h, 0:n], pb[u % 2][:, 0:n], ACT.Exp,
                                             scale=EXP_SCALE).then_inc(s_eb, 1)
                    if u := proj_after(k, 4):
                        n = 4 * u[0] + u[1]
                        act.wait_ge(s_rope, b * 16 + n + 1)
                        if n >= 2:
                            act.wait_ge(s_spread[n % 2], (b * 8 + n // 2) * 32)
                        nc.scalar.activation(rhl[:, n % 2, 0, :], t1[:, n % 2, :], ACT.Copy).then_inc(s_rh, 1)
                    if c := ctx_half(k):
                        n = 2 * c[0] + c[1]
                        act.wait_ge(s_pv, b * 48 + 12 * c[0] + 4 + 8 * c[1])
                        if n:
                            act.wait_ge(s_cf, b * 8 + n)
                        nc.scalar.activation(rec, psum[:, :], ACT.Ln).then_inc(s_ln, 1)
                        act.wait_ge(s_ln, b * 8 + n + 1)
                        nc.scalar.activation(rec, rec, ACT.Exp, scale=-1.0).then_inc(s_rec, 1)
                    if c := ctx_half(k, 4):
                        g, half = c
                        act.wait_ge(s_cf, b * 8 + 2 * g + half + 1)
                        nc.scalar.activation(ch[:, g, half * HALF:(half + 1) * HALF], cf, ACT.Copy).then_inc(s_ch, 1)
                scale_shift(2 * CC)
                scale_shift(3 * CC)
                act.wait_ge(s_out, b * STORED + STORED + 16)

        @block.vector
        def _(dve):
            dve.wait_ge(s_w[4], 16)
            nc.vector.tensor_reduce(sums[:, 0:1], wf_s, AX.XY, ALU.add, apply_absolute_value=True).then_inc(s_abs, 1)
            dve.wait_ge(s_tot, 1)
            nc.vector.tensor_scalar(sums[:, 1:2], pp[:, 0:1], 1.0 / (C * C), Q_EPS, ALU.mult, ALU.add).then_inc(s_abs, 1)
            dve.wait_ge(s_abs, 2)
            nc.vector.tensor_scalar(sums[:, 2:3], sums[:, 1:2], 0.5, None, ALU.mult).then_inc(s_abs, 1)
            nc.vector.tensor_scalar(sums[:, 3:4], sums[:, 1:2], -0.5, None, ALU.mult).then_inc(s_abs, 1)
            dve.wait_ge(s_abs, 4)
            nc.vector.tensor_scalar(wtg, wf_s, sums[:, 2:3], None, ALU.is_gt).then_inc(s_abs, 1)
            dve.wait_ge(s_abs, 5)
            nc.vector.scalar_tensor_tensor(wt[:, :, :], wf_s, sums[:, 3:4], wtg, ALU.is_lt, ALU.subtract).then_inc(s_tern, 1)
            for i in range(4):
                dve.wait_ge(s_wh, i + 1)
                nc.vector.scalar_tensor_tensor(wl[:, i, :, :], stage[i], W_SCALE, wh[:, i, :, :],
                                               ALU.mult, ALU.subtract).then_inc(s_wl, 1)
            with dve.Fori(0, BATCH) as b:
                links = [0]

                def link(ins):
                    links[0] += 1
                    ins.then_inc(s_link, 1)
                    dve.wait_ge(s_link, b * DVE_LINKS + links[0])

                def statistics(bl, n, mul, add):
                    for r in range(4 * bl, 4 * bl + 4):
                        last = nc.vector.bn_stats(stats[:, r, :], xs[:, r, :])
                        last = last.then_inc(s_link, 1)
                        links[0] += 1
                    dve.wait_ge(s_link, b * DVE_LINKS + links[0])
                    nc.vector.memset(hold[:, n - 1:n], 0.0)
                    for r in range(4 * bl, 4 * bl + 4):
                        nc.vector.bn_aggr(mv[:, r, :], stats[:, r, :]).then_inc(s_aggr, 1)
                    dve.wait_ge(s_aggr, b * 24 + 4 * n)
                    cols = slice(4 * bl, 4 * bl + 4)
                    nc.vector.tensor_scalar(var_e[:, cols], mv[:, cols, 1], mul, add, ALU.mult, ALU.add).then_inc(s_var, 1)

                def normalize(bl, n, n_tr):
                    dve.wait_ge(s_rstd, b * 6 + n)
                    if n_tr:
                        dve.wait_ge(*n_tr)
                    for r in range(4 * bl, 4 * bl + 4):
                        nc.vector.tensor_scalar(y[:, bl, r % 4, :], xs[:, r, :], mv[:, r, 0:1], rstd[:, r:r + 1],
                                                ALU.subtract, ALU.mult).then_inc(s_y, 1)

                def f_high(n):
                    for cc in range(CC):
                        dve.wait_ge(s_f, b * 16 + n + cc + 1)
                        if n + cc >= CC:
                            dve.wait_ge(s_ffn, b * 16 + n)
                        nc.vector.tensor_copy(fh[:, cc, :], f[:, cc, :]).then_inc(s_fh, 1)

                def ffn_update(bl, n):
                    for i, r in enumerate(range(4 * bl, 4 * bl + 4)):
                        dve.wait_ge(s_ffn, b * 16 + n + i + 1)
                        dve.wait_ge(s_xb, b * 16 + n + i + 1)
                        nc.vector.scalar_tensor_tensor(xs[:, r, :], pf[r % 2][:, :], -0.5, xs[:, r, :],
                                                       ALU.mult, ALU.add).then_inc(s_xup, 1)

                def ffn(n_r, n_f, y_free):
                    statistics(0, n_r + 1, 1 + LN_EPS, LN_EPS * LN_EPS)
                    statistics(1, n_r + 2, 1 + LN_EPS, LN_EPS * LN_EPS)
                    normalize(0, n_r + 1, y_free)
                    normalize(1, n_r + 2, None)
                    f_high(n_f)
                    ffn_update(0, n_f)
                    f_high(n_f + 4)
                    ffn_update(1, n_f + 4)

                dve.wait_ge(s_x[0], b * 16 + 16)
                dve.wait_ge(s_x[1], b * 16 + 16)
                ffn(0, 0, None)
                for bl in range(BLOCKS):
                    dve.wait_ge(s_xup, b * 16 + 4 * bl + 4)
                    statistics(bl, 3 + bl, 1.0, LN_EPS)
                    normalize(bl, 3 + bl, (s_ytr, b * 16 + 4 * bl + 4))
                for bl in range(BLOCKS):
                    for cc in range(CC):
                        n = CC * bl + cc
                        dve.wait_ge(s_xh, b * 8 + n + 1)
                        cols = slice(bl * HALF, (bl + 1) * HALF)
                        nc.vector.tensor_tensor(xl[:, cc, cols], tr[cc], xh[:, cc, cols], ALU.subtract).then_inc(s_xl, 1)
                for k in range(LAST_STEP):
                    if t := a_unit(k):
                        g, h, i, half = t
                        u = STEPS * g + k - A_START - STEPS * (g + 1)
                        at = A_UNITS * (GH * g + h) + i + 4 * half
                        dve.wait_ge(s_qa, b * 192 + u + 1)
                        n = min(HALF, (i + 1) * P - half * HALF)
                        nc.vector.tensor_reduce(rmax[:, at:at + 1], pa[u % 3][:, 0:n], AX.X, ALU.max,
                                                negate=True).then_inc(s_max, 1)
                    if u := proj_after(k, 1):
                        n = 4 * u[0] + u[1]
                        cols = slice(u[1] // 2 * HALF, (u[1] // 2 + 1) * HALF)
                        dve.wait_ge(s_proj, b * 16 + n + 1)
                        if n >= 2:
                            dve.wait_ge(s_rl, b * 16 + n - 1)
                        nc.vector.tensor_tensor(t1[:, n % 2, :], pp[:, :], cos_s[:, cols], ALU.mult)
                        H2 = P // 2
                        nc.vector.tensor_tensor(rot[0:H2, n % 2, :], pp[H2:P, :], sin_s[H2:P, cols], ALU.mult)
                        nc.vector.tensor_tensor(rot[H2:P, n % 2, :], pp[0:H2, :], sin_s[0:H2, cols], ALU.mult
                                                ).then_inc(s_rot, 1)
                    if e := max_head(k, 1):
                        n = GH * e[0] + e[1]
                        s, at = n % 2, A_UNITS * n
                        dve.wait_ge(s_max, b * 192 + A_UNITS * (n + 1))
                        if n >= 2:
                            dve.wait_ge(s_mtr, b * 16 + n - 1)
                        link(nc.vector.tensor_tensor(rmax[:, at + 4:at + 8], rmax[:, at + 4:at + 8],
                                                     rmax[:, at + 8:at + 12], ALU.min))
                        link(nc.vector.tensor_scalar(mparts[:, s, 0, :], rmax[:, at:at + 8], 1.0 / MAX_SCALE, None, ALU.mult))
                        nc.vector.scalar_tensor_tensor(mparts[:, s, 1, :], rmax[:, at:at + 8], 1.0 / MAX_SCALE,
                                                       mparts[:, s, 0, :], ALU.mult, ALU.subtract).then_inc(s_mp, 1)
                    if e := max_head(k, 4):
                        n = GH * e[0] + e[1]
                        dve.wait_ge(s_mtr, b * 16 + n + 1)
                        if n >= 2:
                            g2, h2 = divmod(n - 2, GH)
                            dve.wait_ge(s_mdma[h2], (b * GROUPS + g2 + 1) * 16)
                        nc.vector.tensor_copy(mrows[:, n % 2, :], pp[0:2 * TILES, 0:P // 2].bitcast(F16)).then_inc(s_mrows, 1)
                    if c := ctx_half(k, 2):
                        n = 2 * c[0] + c[1]
                        dve.wait_ge(s_rec, b * 8 + n + 1)
                        if n:
                            dve.wait_ge(s_cl, b * 8 + n)
                        nc.vector.scalar_tensor_tensor(cf, acc[:, :], CTX_SCALE, rec, ALU.mult, ALU.mult).then_inc(s_cf, 1)
                for r in range(TILES):
                    dve.wait_ge(s_o, b * TILES + r + 1)
                    nc.vector.scalar_tensor_tensor(xs[:, r, :], pw[r % 2][:, :], 1.0 / (CTX_SCALE * W_SCALE),
                                                   xs[:, r, :], ALU.mult, ALU.add).then_inc(s_oup, 1)
                dve.wait_ge(s_oup, b * TILES + TILES)
                ffn(4, 8, None)
                assert links[0] == DVE_LINKS, links
                dve.wait_ge(s_out, b * STORED + STORED + 16)

        @block.tensor
        def _(pe):
            pe.wait_ge(s_pool0, 1)
            pe.wait_ge(s_abs, 1)
            nc.tensor.matmul(pp[:, 0:1], ones[:, :], sums[:, 0:1], start=True, stop=True).then_inc(s_tot, 1)
            pe.wait_ge(s_const, 16 * 7)
            pe.wait_ge(s_tern, 1)
            pe.wait_ge(s_wl, 4)
            pe.wait_ge(s_rows, 32)
            with pe.Fori(0, BATCH) as b:

                def y_chunks(bl, s_done):
                    for cc in range(CC):
                        for r in range(4):
                            last = nc.tensor.transpose(tr[cc][:, r * P:(r + 1) * P], y[:, bl, r, cc * P:(cc + 1) * P],
                                                       ident[:, :])
                        last.then_inc(s_done, 1)

                def ffn_products(bl, n):
                    pe.wait_ge(s_fh, b * 16 + n + CC)
                    pe.wait_ge(s_fl, b * 16 + n + CC)
                    for i in range(4):
                        if n + i >= 2:
                            pe.wait_ge(s_xup, b * 16 + n + i - 1)
                        for a, part in enumerate((fh, fl)):
                            for cc in range(CC):
                                last = nc.tensor.matmul(pf[i % 2][:, :], part[:, cc, i * P:(i + 1) * P], wt[:, cc, :],
                                                        start=(a == 0 and cc == 0), stop=(a == 1 and cc == CC - 1))
                        last.then_inc(s_ffn, 1)

                def ffn(n_y, n_f):
                    pe.wait_ge(s_y, b * 24 + n_y + 4)
                    y_chunks(0, s_ytr)
                    pe.wait_ge(s_y, b * 24 + n_y + 8)
                    pe.wait_ge(s_f, b * 16 + n_f + 4)
                    y_chunks(1, s_ytr)
                    ffn_products(0, n_f)
                    ffn_products(1, n_f + 4)

                ffn(0, 0)
                for bl in range(BLOCKS):
                    pe.wait_ge(s_y, b * 24 + 12 + 4 * bl)
                    if bl:
                        pe.wait_ge(s_xl, b * 8 + 4)
                    else:
                        pe.wait_ge(s_f, b * 16 + 8)
                    y_chunks(bl, s_xtr)

                def products(dst, lhs, rhs, order):
                    for n, (a, c) in enumerate(order):
                        last = nc.tensor.matmul(dst, lhs(a, c), rhs(a, c), start=(n == 0), stop=(n == len(order) - 1))
                    return last

                PASSES = [(0, 0), (1, 0), (0, 1)]
                xp, cp, wp = (xh, xl), (ch, cl), (wh, wl)
                for r in range(TILES):
                    pe.wait_ge(s_xl, b * 8 + 4 * (r // 4) + 4)
                    if r >= 2:
                        pe.wait_ge(s_vs, b * TILES + r - 1)
                    n = 0
                    for pa_, pb_ in PASSES:
                        for cc in range(CC):
                            last = nc.tensor.matmul(pw[r % 2][:, :], xp[pa_][:, cc, r * P:(r + 1) * P],
                                                    wp[pb_][:, 2, cc, :], start=(n == 0), stop=(n == 3 * CC - 1))
                            n += 1
                    last.then_inc(s_v, 1)
                pe.wait_ge(s_vs, b * TILES + TILES)
                evacuated = 0
                transposed = 0
                for k in range(LAST_STEP):
                    if t := b_unit(k):
                        g, st, h, half, j, q0, n = t
                        u = STEPS * g + GH * st + h
                        if st == 0:
                            pe.wait_ge(s_mdma[h], (b * GROUPS + g + 1) * 16)
                        if u >= 2:
                            pe.wait_ge(s_eb, b * 192 + u - 1)
                        nc.tensor.matmul(pb[u % 2][:, 0:n], kst[0:ROWS_B, g % SETS, h, j * P:(j + 1) * P],
                                         qst[0:ROWS_B, g % SETS, h, q0:q0 + n], start=True, stop=True).then_inc(s_qb, 1)
                    if t := a_unit(k):
                        g, h, i, half = t
                        u = STEPS * g + k - A_START - STEPS * (g + 1)
                        if h == 0:
                            for m in range(2 + 2 * (i // 4)):
                                pe.wait_ge(s_stack[m], (b * GROUPS + g + 1) * 16)
                        if u >= 3:
                            pe.wait_ge(s_max, b * 192 + u - 2)
                        n = min(HALF, (i + 1) * P - half * HALF)
                        nc.tensor.matmul(pa[u % 3][:, 0:n], qst[0:ROWS_A, g % SETS, h, i * P:(i + 1) * P],
                                         kst[0:ROWS_A, g % SETS, h, half * HALF:half * HALF + n],
                                         start=True, stop=True).then_inc(s_qa, 1)
                    if u := proj_unit(k):
                        g, m, i = u
                        if i == 0:
                            if evacuated:
                                pe.wait_ge(s_rot, b * 16 + evacuated)
                            if transposed:
                                pe.wait_ge(s_mrows, b * 16 + transposed)
                        for n in (2 * i, 2 * i + 1):
                            a, cc = divmod(n, CC)
                            xw, ww = ((0, 0), (1, 0), (0, 1))[a]
                            last = nc.tensor.matmul(pp[:, :], wp[ww][:, m % 2, cc, g * P:(g + 1) * P],
                                                    xp[xw][:, cc, m // 2 * HALF:(m // 2 + 1) * HALF],
                                                    start=(n == 0), stop=(n == 3 * CC - 1))
                        if i == 5:
                            last.then_inc(s_proj, 1)
                            evacuated += 1
                    if e := max_head(k, 3):
                        n = GH * e[0] + e[1]
                        if evacuated:
                            pe.wait_ge(s_rot, b * 16 + evacuated)
                        pe.wait_ge(s_mp, b * 16 + n + 1)
                        if transposed:
                            pe.wait_ge(s_mrows, b * 16 + transposed)
                        nc.tensor.transpose(pp[0:2 * TILES, 0:P // 2].bitcast(F16),
                                            mparts[:, n % 2, :, :].rearrange("p a t -> p (a t)"),
                                            ident16[:, :]).then_inc(s_mtr, 1)
                        transposed += 1
                    if t := pv_step(k):
                        g, st, half, j, q0, n = t
                        pe.wait_ge(s_eb, b * 192 + STEPS * g + GH * (st + 1))
                        if j == 0 and (g or half):
                            pe.wait_ge(s_cf, b * 8 + 2 * g + half)
                        for h in range(GH):
                            last = nc.tensor.matmul(acc[h * D:(h + 1) * D, q0 - half * HALF:HALF],
                                                    vs[:, j, (GH * g + h) * D:(GH * g + h + 1) * D],
                                                    probs[:, st % 2, h, 0:n], start=(j == 0), stop=(j == 4 * half + 3),
                                                    skip_group_check=True)
                        for h in range(GH):
                            last = nc.tensor.matmul(psum[h * D:(h + 1) * D, q0 - half * HALF:HALF], ones[:, 0:D],
                                                    probs[:, st % 2, h, 0:n], start=(j == 0), stop=(j == 4 * half + 3),
                                                    skip_group_check=True)
                        last.then_inc(s_pv, 1)
                pe.wait_ge(s_mrows, b * 16 + 16)
                pe.wait_ge(s_cl, b * 8 + 8)
                for r in range(TILES):
                    if r >= 2:
                        pe.wait_ge(s_oup, b * TILES + r - 1)
                    n = 0
                    for pa_, pb_ in PASSES:
                        for g in range(GROUPS):
                            last = nc.tensor.matmul(pw[r % 2][:, :], cp[pa_][:, g, r * P:(r + 1) * P],
                                                    wp[pb_][:, 3, g, :], start=(n == 0), stop=(n == 3 * GROUPS - 1))
                            n += 1
                    last.then_inc(s_o, 1)
                ffn(16, 8)
                pe.wait_ge(s_out, b * STORED + STORED + 16)


_INS = ["L0_attn_x", "L0_attn_w_q", "L0_attn_w_k", "L0_attn_w_v", "L0_attn_w_o", "L0_ffn_weight",
        "L0_ffn_bias", "L0_ffn_ln_gamma", "L0_ffn_ln_beta"]


def _constants():
    import numpy as np
    inv = (np.float32(1.0) / np.power(np.float32(10000.0), np.arange(0, D, 2, dtype=np.float32) / np.float32(D))).astype(np.float32)
    freqs = np.outer(np.arange(T, dtype=np.float32), inv).astype(np.float32)
    unit = QK_SCALE / W_SCALE
    pair = np.arange(P) % (P // 2) // GH
    cos = (np.cos(freqs).astype(np.float32)[:, pair].T * np.float32(unit)).astype(np.float32)
    sign = np.where(np.arange(P) < P // 2, 1.0, -1.0).astype(np.float32)[:, None]
    sin = (np.sin(freqs).astype(np.float32)[:, pair].T * sign * np.float32(unit)).astype(np.float32)
    tok = np.arange(T)
    own = np.arange(TILES)[:, None] == tok[None, :] // P
    late = (tok % P >= 64)[None, :]
    q_rows = np.where(own & ~late, 32768.0, 0.0).astype(np.float16)
    k_rows = np.concatenate([np.where(own & late, -32768.0, 0.0), np.full((2, T), MAX_SCALE)]).astype(np.float16)
    return {"cos_t": np.ascontiguousarray(cos), "sin_t": np.ascontiguousarray(sin),
            "ident": np.eye(P, dtype=np.float32), "ident16": np.eye(P, dtype=np.float16),
            "q_rows": q_rows, "k_rows": k_rows}


def _by_halves(w):
    return w.reshape(GROUPS, GH, 2, D // 2, C).transpose(0, 2, 3, 1, 4).reshape(C, C)


def kernel(**inputs):
    import numpy as _np
    import concourse.bacc as _bacc
    from concourse import mybir as _mybir
    from concourse.bass_utils import run_bass_kernel_spmd as _run

    nc = _bacc.Bacc("TRN2", target_bir_lowering=False, num_devices=1)
    nc.disable_value_cache = True
    arrays, args = {}, []
    named = [(n, _np.asarray(inputs[n])) for n in _INS]
    named = [(n, _by_halves(a) if n[-3:] in ("w_q", "w_k") else a) for n, a in named]
    named = [(n, _np.ascontiguousarray(a.T if "_w" in n else a.reshape(CC, P).T if "_ln_" in n else a.reshape(1, C)
                                       if "_bias" in n else a)) for n, a in named] + list(_constants().items())
    for name, a in named:
        arrays[f"in_{name}_dram"] = a
        args.append(nc.dram_tensor(f"in_{name}_dram", a.shape, _mybir.dt.from_np(a.dtype), kind="ExternalInput").ap())
    out = nc.dram_tensor("out_0_dram", (BATCH, T, C), F32, kind="ExternalOutput").ap()
    spread = nc.dram_tensor("spread", (2, 3, P, HALF), F16, kind="Internal").ap()
    macaron(nc, *args, spread, out)
    r = _run(nc, [arrays], core_ids=[0])
    return r.results[0]["out_0_dram"]
```

```python
from contextlib import ExitStack

import concourse.bass as bass
from concourse import mybir

F32 = mybir.dt.float32
F16 = mybir.dt.float16
ALU = mybir.AluOpType
ACT = mybir.ActivationFunctionType
AX = mybir.AxisListType

BATCH, T, C, HEADS = 2, 1024, 512, 16
D = C // HEADS
P = 128
TILES = T // P
CC = C // P
HALF = 512
BLOCKS = T // HALF
GH = P // D
GROUPS = HEADS // GH
SETS = 3
LN_EPS = 1e-5
Q_EPS = 1e-5
W_SCALE = 64.0
QK_SCALE = 16.0
CTX_SCALE = 16.0
EXP_SCALE = float(D) ** -0.5 / (QK_SCALE * QK_SCALE)
MAX_SCALE = 2048.0
MASK_ROW = 3 * D
MAX_ROW = MASK_ROW + TILES
ROWS_A = MAX_ROW
ROWS_B = MAX_ROW + 2

STEPS = 48
A_START, B_START = 6, 18
SUM_LAG, PV_LAG = 5, 7
P_PLACES = 4
A_ORDER = [(i, half) for i in range(TILES) for half in range(i // 4 + 1)]
A_UNITS = len(A_ORDER)
B_ORDER = [(half, j) for half in range(BLOCKS) for j in range(4 * half + 4)]
LAST_STEP = STEPS * (GROUPS + 2) + B_START + PV_LAG + 2
V_STEPS = (18, 30, 42, 48, 66, 78, 90, 96)
X_STEP = 12
O_START = STEPS * (GROUPS + 1) + B_START + 28
DVE_LINKS = 3 * TILES + 2 * HEADS


def macaron(nc, x, w_q, w_k, w_v, w_o, w_f, bias, gamma, beta, cos_t, sin_t, ident_in, ident16_in,
            q_rows, k_rows, spread, out):
    ctx = ExitStack()
    with ctx:
        def sb(name, shape, dt):
            return ctx.enter_context(nc.sbuf_tensor(name, shape, dt))

        def sem(name):
            return ctx.enter_context(nc.semaphore(name))

        xs = sb("xs", [P, TILES, C], F32)
        xh = sb("xh", [P, CC, T], F16)
        xl = sb("xl", [P, CC, T], F16)
        vs = sb("vs", [P, TILES, C], F32)
        ch = sb("ch", [P, GROUPS, T], F16)
        cl = sb("cl", [P, GROUPS, T], F16)
        wh = sb("wh", [P, 4, CC, C], F16)
        wl = sb("wl", [P, 4, CC, C], F16)
        wt = sb("wt", [P, CC, C], F16)
        cos_s = sb("cos_s", [P, T], F32)
        sin_s = sb("sin_s", [P, T], F32)
        qst = sb("qst", [P, SETS, GH, T], F16)
        kst = sb("kst", [P, SETS, GH, T], F16)
        rhl = sb("rhl", [P, 2, 2, HALF], F16)
        t1 = sb("t1", [P, 2, HALF], F32)
        big = sb("big", [P, 32 * 256], F32)
        y = big[:, 0:4096].rearrange("p (b t c) -> p b t c", b=2, t=4)
        f = big[:, 4096:8192].rearrange("p (b c n) -> p b c n", b=BLOCKS, c=CC)
        probs = big[:, 0:8192].rearrange("p (s h n) -> p s h n", s=P_PLACES, h=GH)
        fh, fl = xh, xl
        stage = [xs[:, 4:8, :],
                 qst[:, 0, :, :].rearrange("p h t -> p (h t)").bitcast(F32).rearrange("p (a b) -> p a b", a=4),
                 ch[:, :, :].rearrange("p g t -> p (g t)").bitcast(F32).rearrange("p (a b) -> p a b", a=4),
                 cl[:, :, :].rearrange("p g t -> p (g t)").bitcast(F32).rearrange("p (a b) -> p a b", a=4)]
        wf_s = xs[:, 0:4, :]
        wtg = xl[:, 0:2, :].rearrange("p a t -> p (a t)").rearrange("p (a b) -> p a b", a=4)
        biasb = sb("biasb", [P, C], F32)
        ident = sb("ident", [P, P], F32)
        ident16 = sb("ident16", [P, P], F16)
        ones = sb("ones", [P, P], F32)
        gam = sb("gam", [P, CC], F32)
        bet = sb("bet", [P, CC], F32)
        sums = sb("sums", [P, 4], F32)
        rot = sb("rot", [P, 2, HALF], F32)
        cf = sb("cf", [P, HALF], F32)
        stats = sb("stats", [P, TILES, 6], F32)
        mv = sb("mv", [P, TILES, 2], F32)
        var_e = sb("var_e", [P, TILES], F32)
        half_neg = sb("half_neg", [P, TILES], F32)
        rstd = sb("rstd", [P, TILES], F32)
        rmax = sb("rmax", [P, HEADS * A_UNITS], F32)
        mparts = sb("mparts", [P, 2, 2, TILES], F16)
        mrows = sb("mrows", [2 * TILES, 2, P], F16)
        hold = sb("hold", [P, 6], F32)

        bank = [ctx.enter_context(nc.psum_tensor(f"bank{i}", [P, HALF], F32)) for i in range(8)]
        pa = bank[0:3]
        pb = bank[3:5]
        acc = bank[5]
        psum = bank[6]
        pp = bank[7]
        tr = [[t[:, :] for t in bank[4 * i:4 * i + 4]] for i in range(2)]
        pf = bank[0:4]
        pv = [bank[5], bank[6]]
        pw = [bank[7], bank[2]] * 2 + [bank[7], bank[5]] * 2

        s_const = sem("s_const")
        s_bias = sem("s_bias")
        s_w = [sem(f"s_w{i}") for i in range(5)]
        s_rows = sem("s_rows")
        s_pool0 = sem("s_pool0")
        s_abs = sem("s_abs")
        s_tot = sem("s_tot")
        s_tern = sem("s_tern")
        s_wh = sem("s_wh")
        s_wl = sem("s_wl")
        s_x = [sem(f"s_x{i}") for i in range(BLOCKS)]
        s_link = sem("s_link")
        s_aggr = sem("s_aggr")
        s_var = sem("s_var")
        s_rstd = sem("s_rstd")
        s_y = sem("s_y")
        s_xb = sem("s_xb")
        s_ytr = sem("s_ytr")
        s_f = sem("s_f")
        s_fl = sem("s_fl")
        s_ffn = sem("s_ffn")
        s_xup = sem("s_xup")
        s_xtr = sem("s_xtr")
        s_xh = sem("s_xh")
        s_xl = sem("s_xl")
        s_v = sem("s_v")
        s_vs = sem("s_vs")
        s_proj = sem("s_proj")
        s_rot = sem("s_rot")
        s_spread = [sem(f"s_spread{i}") for i in range(2)]
        s_rope = sem("s_rope")
        s_rh = sem("s_rh")
        s_rl = sem("s_rl")
        s_stack = [sem(f"s_stack{i}") for i in range(4)]
        s_qa = sem("s_qa")
        s_max = sem("s_max")
        s_mp = sem("s_mp")
        s_mtr = sem("s_mtr")
        s_mrows = sem("s_mrows")
        s_mdma = [sem(f"s_mdma{i}") for i in range(GH)]
        s_qb = sem("s_qb")
        s_eb = sem("s_eb")
        s_sum = sem("s_sum")
        s_pv = sem("s_pv")
        s_ln = sem("s_ln")
        s_rec = sem("s_rec")
        s_cf = sem("s_cf")
        s_ch = sem("s_ch")
        s_cl = sem("s_cl")
        s_o = sem("s_o")
        s_oup = sem("s_oup")
        s_out = sem("s_out")

        STORED = 16 * TILES
        block = ctx.enter_context(nc.Block())

        def proj_unit(k, lag=0):
            g, r = divmod(k - lag, STEPS)
            if 0 <= g < GROUPS and r % A_UNITS < 6:
                return g, r // A_UNITS, r % A_UNITS

        def proj_after(k, lag):
            u = proj_unit(k, lag)
            return u[:2] if u and u[2] == 5 else None

        def v_unit(k, lag=0):
            for r, at in enumerate(V_STEPS):
                if at <= k - lag < at + 6:
                    return r, k - lag - at

        def o_unit(k, lag=0):
            r, i = divmod(k - lag - O_START, 6)
            if 0 <= r < 4:
                return r, i

        def a_unit(k):
            g, r = divmod(k - A_START, STEPS)
            if 1 <= g <= GROUPS:
                return g - 1, r // A_UNITS, *A_ORDER[r % A_UNITS]

        def max_head(k, lag):
            t = a_unit(k - lag)
            return t[:2] if t and t[2:] == A_ORDER[-1] else None

        def b_unit(k):
            g, r = divmod(k - B_START, STEPS)
            if 2 <= g < GROUPS + 2:
                half, j = B_ORDER[r // GH]
                q0 = max(half * HALF, j * P)
                return g - 2, r // GH, r % GH, half, j, q0, (half + 1) * HALF - q0

        def pv_step(k, lag):
            t = b_unit(k - lag)
            return (t[0], t[1], *t[3:]) if t and t[2] == 0 else None

        def ctx_half(k, lag=1):
            s = pv_step(k - lag, PV_LAG)
            return (s[0], s[2]) if s and s[3] == 4 * s[2] + 3 else None

        @block.sync
        def _(sp):
            sp.dma_start(wf_s, w_f.rearrange("(a p) o -> p a o", p=P)).then_inc(s_w[4], 16)
            sp.sem_inc(s_o, 1)
            sp.sem_inc(s_out, 16)
            with sp.Fori(0, BATCH) as b:
                sp.wait_ge(s_o, b * TILES + 1)
                for bl in range(BLOCKS):
                    sp.dma_start(vs[:, 4 * bl:4 * bl + 4, :],
                                 x[bass.ds(b, 1), bl * HALF:(bl + 1) * HALF, :].rearrange("b (t p) c -> p (b t) c", p=P)
                                 ).then_inc(s_x[bl], 16)
                for k in range(LAST_STEP):
                    if u := proj_after(k, 8):
                        g, m = u
                        n = 4 * g + m
                        sp.wait_ge(s_rl, b * 16 + n + 1)
                        if n >= 2:
                            g2, m2 = divmod(n - 2, 4)
                            sp.wait_ge(s_stack[m2], (b * GROUPS + g2 + 1) * 16)
                        low, again = (slice(0, 3, 2), 1) if m % 2 else (slice(0, 2), 2)
                        sp.dma_start(spread[n % 2, low].rearrange("a p t -> p a t"), rhl[:, n % 2, :, :]
                                     ).then_inc(s_spread[n % 2], 16)
                        sp.dma_start(spread[n % 2, again], rhl[:, n % 2, 0, :]).then_inc(s_spread[n % 2], 16)
                    if u := proj_after(k, 11):
                        g, m = u
                        n = 4 * g + m
                        dst, cols = (kst if m % 2 else qst), slice(m // 2 * HALF, (m // 2 + 1) * HALF)
                        sp.wait_ge(s_spread[n % 2], (b * 8 + n // 2 + 1) * 32)
                        if g >= SETS:
                            sp.wait_ge(s_qb, b * STEPS * GROUPS + STEPS * (g - SETS + 1))
                        sp.dma_start(dst[0:MASK_ROW, g % SETS, :, cols],
                                     spread[n % 2].rearrange("a (d h) t -> (a d) h t", h=GH)).then_inc(s_stack[m], 16)
                    if e := max_head(k, 7):
                        g, h = e
                        n = GH * g + h
                        sp.wait_ge(s_mrows, b * 16 + n + 1)
                        sp.dma_start(qst[MAX_ROW:ROWS_B, g % SETS, h, :], mrows[:, n % 2, :]).then_inc(s_mdma[h], 16)

        @block.gpsimd
        def _(pool):
            pool.memset(ones[:, :], 1.0).then_inc(s_pool0, 1)
            pool.memset(half_neg[:, :], -0.5).then_inc(s_pool0, 1)
            pool.wait_ge(s_pool0, 2)
            pool.wait_ge(s_bias, 16)
            pool.tensor_scalar(biasb[:, :], biasb[:, :], 0.5, None, ALU.mult).then_inc(s_pool0, 1)
            pool.wait_ge(s_pool0, 3)
            with pool.Fori(0, BATCH) as b:

                def rstd_of(bl, i):
                    cols = slice(4 * bl, 4 * bl + 4)
                    pool.wait_ge(s_var, b * 6 + i + 1)
                    pool.tensor_tensor(rstd[:, cols], var_e[:, cols], half_neg[:, cols], ALU.pow).then_inc(s_rstd, 1)

                def add_bias(bl, n, rows):
                    pool.wait_ge(s_y, b * 24 + n)
                    for r in range(4 * bl, 4 * bl + 4):
                        pool.tensor_tensor(xs[:, r, :], rows[:, r, :], biasb[:, :], ALU.add).then_inc(s_xb, 1)

                rstd_of(0, 0)
                rstd_of(1, 1)
                pool.wait_ge(s_out, b * STORED + 16)
                add_bias(0, 4, vs)
                add_bias(1, 8, vs)
                rstd_of(0, 2)
                rstd_of(1, 3)
                for k in range(LAST_STEP):
                    if u := proj_after(k, 3):
                        n = 4 * u[0] + u[1]
                        pool.wait_ge(s_rot, b * 16 + n + 1)
                        pool.tensor_tensor(t1[:, n % 2, :], t1[:, n % 2, :], rot[:, n % 2, :], ALU.add).then_inc(s_rope, 1)
                    if u := proj_after(k, 7):
                        n = 4 * u[0] + u[1]
                        pool.wait_ge(s_rh, b * 16 + n + 1)
                        pool.tensor_tensor(rhl[:, n % 2, 1, :], t1[:, n % 2, :], rhl[:, n % 2, 0, :], ALU.subtract
                                           ).then_inc(s_rl, 1)
                    if c := ctx_half(k, 5):
                        g, half = c
                        cols = slice(half * HALF, (half + 1) * HALF)
                        pool.wait_ge(s_ch, b * 8 + 2 * g + half + 1)
                        pool.tensor_tensor(cl[:, g, cols], cf[:, :], ch[:, g, cols], ALU.subtract).then_inc(s_cl, 1)
                for bl in range(BLOCKS):
                    rstd_of(bl, 4 + bl)
                    add_bias(bl, 20 + 4 * bl, xs)
                pool.wait_ge(s_xup, b * 16 + 16)

        @block.scalar
        def _(act):
            nc.scalar.preload_act_table_set("natural_log_exp_and_others")
            for i, w in enumerate((w_q, w_k, w_v, w_o)):
                act.dma_start(stage[i], w.rearrange("(a p) o -> p a o", p=P)).then_inc(s_w[i], 16)
            act.dma_start(biasb[:, :], bias.broadcast_to([P, C])).then_inc(s_bias, 16)
            act.dma_start(ident[:, :], ident_in).then_inc(s_const, 16)
            act.dma_start(ident16[:, :], ident16_in).then_inc(s_const, 16)
            act.dma_start(gam[:, :], gamma).then_inc(s_const, 16)
            act.dma_start(bet[:, :], beta).then_inc(s_const, 16)
            act.dma_start(cos_s[:, :], cos_t).then_inc(s_const, 16)
            act.dma_start(sin_s[:, :], sin_t).then_inc(s_const, 16)
            for i in range(4):
                act.wait_ge(s_w[i], 16)
                nc.scalar.activation(wh[:, i, :, :], stage[i], ACT.Copy, scale=W_SCALE).then_inc(s_wh, 1)
            act.wait_ge(s_wl, 2)
            for stack, first, last, rows in ((qst, MASK_ROW, MAX_ROW, q_rows), (kst, MASK_ROW, ROWS_B, k_rows)):
                act.dma_start(stack[first:last, :, :, :].rearrange("r s h t -> r (s h) t"),
                              rows.rearrange("r (a t) -> r a t", a=1).broadcast_to([last - first, SETS * GH, T])
                              ).then_inc(s_rows, 16)
            with act.Fori(0, BATCH) as b:

                def scale_shift(n_t):
                    bl = n_t // CC % 2
                    cols = slice(bl * HALF, (bl + 1) * HALF)
                    for cc in range(CC):
                        act.wait_ge(s_ytr, b * 16 + n_t + cc + 1)
                        nc.scalar.activation(fh[:, cc, cols], tr[bl][cc], ACT.Identity, bias=bet[:, cc:cc + 1],
                                             scale=gam[:, cc:cc + 1])
                        nc.scalar.activation(f[:, bl, cc, :], tr[bl][cc], ACT.Identity, bias=bet[:, cc:cc + 1],
                                             scale=gam[:, cc:cc + 1]).then_inc(s_f, 1)

                def x_high(bl):
                    for cc in range(CC):
                        act.wait_ge(s_xtr, b * 8 + CC * bl + cc + 1)
                        nc.scalar.activation(xh[:, cc, bl * HALF:(bl + 1) * HALF], tr[1 - bl][cc], ACT.Copy).then_inc(s_xh, 1)

                act.wait_ge(s_const, 16 * 6)
                scale_shift(0)
                scale_shift(CC)
                x_high(0)
                for k in range(LAST_STEP):
                    if k == X_STEP:
                        x_high(1)
                    if (v := v_unit(k, 1)) and v[1] == 5:
                        r = v[0]
                        act.wait_ge(s_v, b * TILES + r + 1)
                        nc.scalar.activation(vs[:, r, :], pv[r % 2][:, :], ACT.Copy, scale=1.0 / W_SCALE).then_inc(s_vs, 1)
                    if t := b_unit(k):
                        g, st, h, half, j, q0, n = t
                        u = STEPS * g + GH * st + h
                        act.wait_ge(s_qb, b * 192 + u + 1)
                        if 12 * g + st >= P_PLACES:
                            act.wait_ge(s_pv, b * 48 + 12 * g + st + 1 - P_PLACES)
                        nc.scalar.activation(probs[:, st % P_PLACES, h, 0:n], pb[u % 2][:, 0:n], ACT.Exp,
                                             scale=EXP_SCALE).then_inc(s_eb, 1)
                    if e := max_head(k, 6):
                        n = GH * e[0] + e[1]
                        act.wait_ge(s_mtr, b * 16 + n + 1)
                        if n >= 2:
                            g2, h2 = divmod(n - 2, GH)
                            act.wait_ge(s_mdma[h2], (b * GROUPS + g2 + 1) * 16)
                        nc.scalar.activation(mrows[:, n % 2, :], pp[0:2 * TILES, 0:P // 2].bitcast(F16), ACT.Copy).then_inc(s_mrows, 1)
                    if u := proj_after(k, 6):
                        n = 4 * u[0] + u[1]
                        act.wait_ge(s_rope, b * 16 + n + 1)
                        if n >= 2:
                            act.wait_ge(s_spread[n % 2], (b * 8 + n // 2) * 32)
                        nc.scalar.activation(rhl[:, n % 2, 0, :], t1[:, n % 2, :], ACT.Copy).then_inc(s_rh, 1)
                    if c := ctx_half(k, 0):
                        n = 2 * c[0] + c[1]
                        act.wait_ge(s_sum, b * 48 + 12 * c[0] + 4 + 8 * c[1])
                        if n:
                            act.wait_ge(s_cl, b * 8 + n)
                        nc.scalar.activation(cf[:, :], psum[:, :], ACT.Ln).then_inc(s_ln, 1)
                        act.wait_ge(s_ln, b * 8 + n + 1)
                        nc.scalar.activation(cf[:, :], cf[:, :], ACT.Exp, scale=-1.0).then_inc(s_rec, 1)
                    if c := ctx_half(k, 4):
                        g, half = c
                        act.wait_ge(s_cf, b * 8 + 2 * g + half + 1)
                        nc.scalar.activation(ch[:, g, half * HALF:(half + 1) * HALF], cf[:, :], ACT.Copy).then_inc(s_ch, 1)
                scale_shift(2 * CC)
                scale_shift(3 * CC)
                for r in range(TILES):
                    act.wait_ge(s_xup, b * 16 + TILES + r + 1)
                    act.dma_start(out[bass.ds(b, 1), r * P:(r + 1) * P, :].rearrange("b p c -> p (b c)"), xs[:, r, :]).then_inc(s_out, 16)
            act.wait_ge(s_out, BATCH * STORED + 16)

        @block.vector
        def _(dve):
            dve.wait_ge(s_w[4], 16)
            nc.vector.tensor_reduce(sums[:, 0:1], wf_s, AX.XY, ALU.add, apply_absolute_value=True).then_inc(s_abs, 1)
            dve.wait_ge(s_tot, 1)
            nc.vector.tensor_scalar(sums[:, 1:2], pp[:, 0:1], 1.0 / (C * C), Q_EPS, ALU.mult, ALU.add).then_inc(s_abs, 1)
            dve.wait_ge(s_abs, 2)
            nc.vector.tensor_scalar(sums[:, 2:3], sums[:, 1:2], 0.5, None, ALU.mult).then_inc(s_abs, 1)
            nc.vector.tensor_scalar(sums[:, 3:4], sums[:, 1:2], -0.5, None, ALU.mult).then_inc(s_abs, 1)
            dve.wait_ge(s_abs, 4)
            nc.vector.tensor_scalar(wtg, wf_s, sums[:, 2:3], None, ALU.is_gt).then_inc(s_abs, 1)
            dve.wait_ge(s_abs, 5)
            nc.vector.scalar_tensor_tensor(wt[:, :, :], wf_s, sums[:, 3:4], wtg, ALU.is_lt, ALU.subtract).then_inc(s_tern, 1)
            for i in range(4):
                dve.wait_ge(s_wh, i + 1)
                nc.vector.scalar_tensor_tensor(wl[:, i, :, :], stage[i], W_SCALE, wh[:, i, :, :],
                                               ALU.mult, ALU.subtract).then_inc(s_wl, 1)
            with dve.Fori(0, BATCH) as b:
                links = [0]

                def link(ins):
                    links[0] += 1
                    ins.then_inc(s_link, 1)
                    dve.wait_ge(s_link, b * DVE_LINKS + links[0])

                def statistics(bl, n, mul, add, rows=xs):
                    for r in range(4 * bl, 4 * bl + 4):
                        last = nc.vector.bn_stats(stats[:, r, :], rows[:, r, :])
                        last = last.then_inc(s_link, 1)
                        links[0] += 1
                    dve.wait_ge(s_link, b * DVE_LINKS + links[0])
                    nc.vector.memset(hold[:, n - 1:n], 0.0)
                    for r in range(4 * bl, 4 * bl + 4):
                        nc.vector.bn_aggr(mv[:, r, :], stats[:, r, :]).then_inc(s_aggr, 1)
                    dve.wait_ge(s_aggr, b * 24 + 4 * n)
                    cols = slice(4 * bl, 4 * bl + 4)
                    nc.vector.tensor_scalar(var_e[:, cols], mv[:, cols, 1], mul, add, ALU.mult, ALU.add).then_inc(s_var, 1)

                def normalize(bl, n, n_tr, rows=xs):
                    dve.wait_ge(s_rstd, b * 6 + n)
                    if n_tr:
                        dve.wait_ge(*n_tr)
                    for r in range(4 * bl, 4 * bl + 4):
                        nc.vector.tensor_scalar(y[:, bl, r % 4, :], rows[:, r, :], mv[:, r, 0:1], rstd[:, r:r + 1],
                                                ALU.subtract, ALU.mult).then_inc(s_y, 1)

                def f_low(n):
                    bl = n // CC % 2
                    cols = slice(bl * HALF, (bl + 1) * HALF)
                    for cc in range(CC):
                        dve.wait_ge(s_f, b * 16 + n + cc + 1)
                        nc.vector.tensor_tensor(fl[:, cc, cols], f[:, bl, cc, :], fh[:, cc, cols], ALU.subtract
                                                ).then_inc(s_fl, 1)

                def ffn_update(bl, n):
                    for i, r in enumerate(range(4 * bl, 4 * bl + 4)):
                        dve.wait_ge(s_ffn, b * 16 + n + i + 1)
                        dve.wait_ge(s_xb, b * 16 + n + i + 1)
                        nc.vector.scalar_tensor_tensor(xs[:, r, :], pf[r % 4][:, :], -0.5, xs[:, r, :],
                                                       ALU.mult, ALU.add).then_inc(s_xup, 1)

                def x_low(bl):
                    for cc in range(CC):
                        dve.wait_ge(s_xh, b * 8 + CC * bl + cc + 1)
                        cols = slice(bl * HALF, (bl + 1) * HALF)
                        nc.vector.tensor_tensor(xl[:, cc, cols], tr[1 - bl][cc], xh[:, cc, cols], ALU.subtract).then_inc(s_xl, 1)

                def attention_update(r):
                    dve.wait_ge(s_o, b * TILES + r + 2)
                    nc.vector.scalar_tensor_tensor(xs[:, r, :], pw[r][:, :], 1.0 / (CTX_SCALE * W_SCALE),
                                                   xs[:, r, :], ALU.mult, ALU.add).then_inc(s_oup, 1)

                TWICE = (1 + LN_EPS, LN_EPS * LN_EPS)
                for bl in range(BLOCKS):
                    dve.wait_ge(s_x[bl], b * 16 + 16)
                    statistics(bl, 1 + bl, *TWICE, vs)
                for bl in range(BLOCKS):
                    normalize(bl, 1 + bl, None, vs)
                for bl in range(BLOCKS):
                    f_low(4 * bl)
                for bl in range(BLOCKS):
                    ffn_update(bl, 4 * bl)
                    dve.wait_ge(s_xup, b * 16 + 4 * bl + 4)
                    statistics(bl, 3 + bl, 1.0, LN_EPS)
                    if bl:
                        x_low(0)
                    normalize(bl, 3 + bl, (s_ytr, b * 16 + 4 * bl + 4))
                for k in range(LAST_STEP):
                    if k == X_STEP + 1:
                        x_low(1)
                    if t := a_unit(k):
                        g, h, i, half = t
                        u = STEPS * g + k - A_START - STEPS * (g + 1)
                        at = A_UNITS * (GH * g + h) + i + 4 * half
                        dve.wait_ge(s_qa, b * 192 + u + 1)
                        n = min(HALF, (i + 1) * P - half * HALF)
                        nc.vector.tensor_reduce(rmax[:, at:at + 1], pa[u % 3][:, 0:n], AX.X, ALU.max,
                                                negate=True).then_inc(s_max, 1)
                    if u := proj_after(k, 1):
                        n = 4 * u[0] + u[1]
                        cols = slice(u[1] // 2 * HALF, (u[1] // 2 + 1) * HALF)
                        dve.wait_ge(s_proj, b * 16 + n + 1)
                        if n >= 2:
                            dve.wait_ge(s_rl, b * 16 + n - 1)
                        nc.vector.tensor_tensor(t1[:, n % 2, :], pp[:, :], cos_s[:, cols], ALU.mult)
                    for lag, first in ((1, 0), (2, P // 2)):
                        if u := proj_after(k, lag):
                            n, other = 4 * u[0] + u[1], P // 2 - first
                            cols = slice(u[1] // 2 * HALF, (u[1] // 2 + 1) * HALF)
                            last = nc.vector.tensor_tensor(rot[first:first + P // 2, n % 2, :], pp[other:other + P // 2, :],
                                                           sin_s[other:other + P // 2, cols], ALU.mult)
                            if first:
                                last.then_inc(s_rot, 1)
                    if (o := o_unit(k, 1)) and o[1] == 5:
                        attention_update(o[0])
                    if e := max_head(k, 1):
                        n = GH * e[0] + e[1]
                        s, at = n % 2, A_UNITS * n
                        dve.wait_ge(s_max, b * 192 + A_UNITS * (n + 1))
                        if n >= 2:
                            dve.wait_ge(s_mtr, b * 16 + n - 1)
                        link(nc.vector.tensor_tensor(rmax[:, at + 4:at + 8], rmax[:, at + 4:at + 8],
                                                     rmax[:, at + 8:at + 12], ALU.min))
                        link(nc.vector.tensor_scalar(mparts[:, s, 0, :], rmax[:, at:at + 8], 1.0 / MAX_SCALE, None, ALU.mult))
                        nc.vector.scalar_tensor_tensor(mparts[:, s, 1, :], rmax[:, at:at + 8], 1.0 / MAX_SCALE,
                                                       mparts[:, s, 0, :], ALU.mult, ALU.subtract).then_inc(s_mp, 1)
                    if c := ctx_half(k, 2):
                        n = 2 * c[0] + c[1]
                        dve.wait_ge(s_rec, b * 8 + n + 1)
                        dve.wait_ge(s_pv, b * 48 + 12 * c[0] + 4 + 8 * c[1])
                        nc.vector.scalar_tensor_tensor(cf[:, :], acc[:, :], CTX_SCALE, cf[:, :], ALU.mult, ALU.mult).then_inc(s_cf, 1)
                dve.wait_ge(s_oup, b * TILES + 4)
                statistics(0, 5, *TWICE)
                normalize(0, 5, None)
                attention_update(4)
                attention_update(5)
                attention_update(6)
                f_low(8)
                attention_update(7)
                dve.wait_ge(s_oup, b * TILES + TILES)
                statistics(1, 6, *TWICE)
                normalize(1, 6, None)
                ffn_update(0, 8)
                f_low(12)
                ffn_update(1, 12)
                assert links[0] == DVE_LINKS, links

        @block.tensor
        def _(pe):
            pe.wait_ge(s_pool0, 1)
            pe.wait_ge(s_abs, 1)
            nc.tensor.matmul(pp[:, 0:1], ones[:, :], sums[:, 0:1], start=True, stop=True).then_inc(s_tot, 1)
            pe.wait_ge(s_const, 16 * 6)
            pe.wait_ge(s_tern, 1)
            pe.wait_ge(s_wl, 4)
            pe.wait_ge(s_rows, 32)
            with pe.Fori(0, BATCH) as b:

                def y_chunks(bl, banks, s_done):
                    for cc in range(CC):
                        for r in range(4):
                            last = nc.tensor.transpose(tr[banks][cc][:, r * P:(r + 1) * P], y[:, bl, r, cc * P:(cc + 1) * P],
                                                       ident[:, :])
                        last.then_inc(s_done, 1)

                def ffn_products(bl, n):
                    pe.wait_ge(s_fl, b * 16 + n + CC)
                    for i in range(4):
                        if bl:
                            pe.wait_ge(s_xup, b * 16 + n + i - 3)
                        for a, part in enumerate((fh, fl)):
                            for cc in range(CC):
                                last = nc.tensor.matmul(pf[i][:, :], part[:, cc, (4 * bl + i) * P:(4 * bl + i + 1) * P], wt[:, cc, :],
                                                        start=(a == 0 and cc == 0), stop=(a == 1 and cc == CC - 1))
                        last.then_inc(s_ffn, 1)

                def output_products(r, ns):
                    for n in ns:
                        a, g = divmod(n, GROUPS)
                        last = nc.tensor.matmul(pw[r][:, :], (ch, cl)[PASSES[a][0]][:, g, r * P:(r + 1) * P],
                                                (wh, wl)[PASSES[a][1]][:, 3, g, :], start=(n == 0), stop=(n == 3 * GROUPS - 1))
                    if ns[-1] == 3 * GROUPS - 1:
                        last.then_inc(s_o, 1)

                PASSES = [(0, 0), (1, 0), (0, 1)]
                pe.wait_ge(s_y, b * 24 + 4)
                y_chunks(0, 0, s_ytr)
                pe.wait_ge(s_y, b * 24 + 8)
                y_chunks(1, 1, s_ytr)
                ffn_products(0, 0)
                ffn_products(1, 4)
                pe.wait_ge(s_y, b * 24 + 12)
                y_chunks(0, 1, s_xtr)

                xp, wp = (xh, xl), (wh, wl)
                evacuated = 0
                transposed = 0
                for k in range(LAST_STEP):
                    if k == X_STEP:
                        pe.wait_ge(s_y, b * 24 + 16)
                        y_chunks(1, 0, s_xtr)
                    if t := b_unit(k):
                        g, st, h, half, j, q0, n = t
                        u = STEPS * g + GH * st + h
                        if st == 0:
                            pe.wait_ge(s_mdma[h], (b * GROUPS + g + 1) * 16)
                        if u >= 2:
                            pe.wait_ge(s_eb, b * 192 + u - 1)
                        nc.tensor.matmul(pb[u % 2][:, 0:n], kst[0:ROWS_B, g % SETS, h, j * P:(j + 1) * P],
                                         qst[0:ROWS_B, g % SETS, h, q0:q0 + n], start=True, stop=True).then_inc(s_qb, 1)
                    if t := a_unit(k):
                        g, h, i, half = t
                        u = STEPS * g + k - A_START - STEPS * (g + 1)
                        if h == 0:
                            for m in range(2 + 2 * (i // 4)):
                                pe.wait_ge(s_stack[m], (b * GROUPS + g + 1) * 16)
                        if u >= 3:
                            pe.wait_ge(s_max, b * 192 + u - 2)
                        n = min(HALF, (i + 1) * P - half * HALF)
                        nc.tensor.matmul(pa[u % 3][:, 0:n], qst[0:ROWS_A, g % SETS, h, i * P:(i + 1) * P],
                                         kst[0:ROWS_A, g % SETS, h, half * HALF:half * HALF + n],
                                         start=True, stop=True).then_inc(s_qa, 1)
                    if u := proj_unit(k):
                        g, m, i = u
                        if i == 0:
                            if g == 0:
                                pe.wait_ge(s_xl, b * 8 + 4 * (m // 2) + 4)
                            if evacuated:
                                pe.wait_ge(s_rot, b * 16 + evacuated)
                            if transposed:
                                pe.wait_ge(s_mrows, b * 16 + transposed)
                        for n in (2 * i, 2 * i + 1):
                            a, cc = divmod(n, CC)
                            xw, ww = PASSES[a]
                            last = nc.tensor.matmul(pp[:, :], wp[ww][:, m % 2, cc, g * P:(g + 1) * P],
                                                    xp[xw][:, cc, m // 2 * HALF:(m // 2 + 1) * HALF],
                                                    start=(n == 0), stop=(n == 3 * CC - 1))
                        if i == 5:
                            last.then_inc(s_proj, 1)
                            evacuated += 1
                    if o := o_unit(k):
                        r, i = o
                        if i == 0 and r == 0:
                            pe.wait_ge(s_mrows, b * 16 + 16)
                            pe.wait_ge(s_max, b * 192 + 192)
                            pe.wait_ge(s_cl, b * 8 + 7)
                        if i == 0 and r >= 2:
                            pe.wait_ge(s_oup, b * TILES + r - 1)
                        output_products(r, (2 * i, 2 * i + 1))
                    if v := v_unit(k):
                        r, i = v
                        if i == 0:
                            if r == 0:
                                pe.wait_ge(s_xl, b * 8 + 4)
                            if r >= 2:
                                pe.wait_ge(s_vs, b * TILES + r - 1)
                            if r >= 4:
                                pe.wait_ge(s_xl, b * 8 + 8)
                        for n in (2 * i, 2 * i + 1):
                            a, cc = divmod(n, CC)
                            last = nc.tensor.matmul(pv[r % 2][:, :], xp[PASSES[a][0]][:, cc, r * P:(r + 1) * P],
                                                    wp[PASSES[a][1]][:, 2, cc, :], start=(n == 0), stop=(n == 3 * CC - 1))
                        if i == 5:
                            last.then_inc(s_v, 1)
                    if e := max_head(k, 5):
                        n = GH * e[0] + e[1]
                        if evacuated:
                            pe.wait_ge(s_rot, b * 16 + evacuated)
                        pe.wait_ge(s_mp, b * 16 + n + 1)
                        if transposed:
                            pe.wait_ge(s_mrows, b * 16 + transposed)
                        nc.tensor.transpose(pp[0:2 * TILES, 0:P // 2].bitcast(F16),
                                            mparts[:, n % 2, :, :].rearrange("p a t -> p (a t)"),
                                            ident16[:, :]).then_inc(s_mtr, 1)
                        transposed += 1
                    if t := pv_step(k, SUM_LAG):
                        g, st, half, j, q0, n = t
                        pe.wait_ge(s_eb, b * 192 + STEPS * g + GH * (st + 1))
                        if st == 0 and g == 0:
                            pe.wait_ge(s_vs, b * TILES + TILES)
                        if j == 0 and (g or half):
                            pe.wait_ge(s_ln, b * 8 + 2 * g + half)
                        for h in range(GH):
                            last = nc.tensor.matmul(psum[h * D:(h + 1) * D, q0 - half * HALF:HALF], ones[:, 0:D],
                                                    probs[:, st % P_PLACES, h, 0:n], start=(j == 0), stop=(j == 4 * half + 3),
                                                    skip_group_check=True)
                        last.then_inc(s_sum, 1)
                    if t := pv_step(k, PV_LAG):
                        g, st, half, j, q0, n = t
                        if j == 0 and (g or half):
                            pe.wait_ge(s_cf, b * 8 + 2 * g + half)
                        for h in range(GH):
                            last = nc.tensor.matmul(acc[h * D:(h + 1) * D, q0 - half * HALF:HALF],
                                                    vs[:, j, (GH * g + h) * D:(GH * g + h + 1) * D],
                                                    probs[:, st % P_PLACES, h, 0:n], start=(j == 0), stop=(j == 4 * half + 3),
                                                    skip_group_check=True)
                        last.then_inc(s_pv, 1)
                pe.wait_ge(s_cl, b * 8 + 8)
                for r in range(4, TILES):
                    pe.wait_ge(s_oup, b * TILES + r - 1)
                    output_products(r, range(3 * GROUPS))
                    if r == 5:
                        pe.wait_ge(s_y, b * 24 + 20)
                        y_chunks(0, 0, s_ytr)
                ffn_products(0, 8)
                pe.wait_ge(s_y, b * 24 + 24)
                y_chunks(1, 1, s_ytr)
                ffn_products(1, 12)
                pe.wait_ge(s_xup, b * 16 + 16)


_INS = ["L0_attn_x", "L0_attn_w_q", "L0_attn_w_k", "L0_attn_w_v", "L0_attn_w_o", "L0_ffn_weight",
        "L0_ffn_bias", "L0_ffn_ln_gamma", "L0_ffn_ln_beta"]


def _constants():
    import numpy as np
    inv = (np.float32(1.0) / np.power(np.float32(10000.0), np.arange(0, D, 2, dtype=np.float32) / np.float32(D))).astype(np.float32)
    freqs = np.outer(np.arange(T, dtype=np.float32), inv).astype(np.float32)
    unit = QK_SCALE / W_SCALE
    pair = np.arange(P) % (P // 2) // GH
    cos = (np.cos(freqs).astype(np.float32)[:, pair].T * np.float32(unit)).astype(np.float32)
    sign = np.where(np.arange(P) < P // 2, 1.0, -1.0).astype(np.float32)[:, None]
    sin = (np.sin(freqs).astype(np.float32)[:, pair].T * sign * np.float32(unit)).astype(np.float32)
    tok = np.arange(T)
    own = np.arange(TILES)[:, None] == tok[None, :] // P
    late = (tok % P >= 64)[None, :]
    q_rows = np.where(own & ~late, 32768.0, 0.0).astype(np.float16)
    k_rows = np.concatenate([np.where(own & late, -32768.0, 0.0), np.full((2, T), MAX_SCALE)]).astype(np.float16)
    return {"cos_t": np.ascontiguousarray(cos), "sin_t": np.ascontiguousarray(sin),
            "ident": np.eye(P, dtype=np.float32), "ident16": np.eye(P, dtype=np.float16),
            "q_rows": q_rows, "k_rows": k_rows}


def _by_halves(w):
    return w.reshape(GROUPS, GH, 2, D // 2, C).transpose(0, 2, 3, 1, 4).reshape(C, C)


def kernel(**inputs):
    import numpy as _np
    import concourse.bacc as _bacc
    from concourse import mybir as _mybir
    from concourse.bass_utils import run_bass_kernel_spmd as _run

    nc = _bacc.Bacc("TRN2", target_bir_lowering=False, num_devices=1)
    nc.disable_value_cache = True
    arrays, args = {}, []
    named = [(n, _np.asarray(inputs[n])) for n in _INS]
    named = [(n, _by_halves(a) if n[-3:] in ("w_q", "w_k") else a) for n, a in named]
    named = [(n, _np.ascontiguousarray(a.T if "_w" in n else a.reshape(CC, P).T if "_ln_" in n else a.reshape(1, C)
                                       if "_bias" in n else a)) for n, a in named] + list(_constants().items())
    for name, a in named:
        arrays[f"in_{name}_dram"] = a
        args.append(nc.dram_tensor(f"in_{name}_dram", a.shape, _mybir.dt.from_np(a.dtype), kind="ExternalInput").ap())
    out = nc.dram_tensor("out_0_dram", (BATCH, T, C), F32, kind="ExternalOutput").ap()
    spread = nc.dram_tensor("spread", (2, 3, P, HALF), F16, kind="Internal").ap()
    macaron(nc, *args, spread, out)
    r = _run(nc, [arrays], core_ids=[0])
    return r.results[0]["out_0_dram"]
```
